# Optimizing a Trainium2 kernel written in Bass

```python
import numpy as np
import jax
import jax.numpy as jnp

def _softmax(x, axis=-1):
    return jax.nn.softmax(x, axis=axis)

def _gelu(x):
    return jax.nn.gelu(x, approximate=True)

def _silu(x):
    return jax.nn.silu(x)

def _sigmoid(x):
    return jax.nn.sigmoid(x)

def _layernorm(x, axis=-1, eps=1e-05):
    m = jnp.mean(x, axis=axis, keepdims=True)
    v = jnp.var(x, axis=axis, keepdims=True)
    return (x - m) / jnp.sqrt(v + eps)

def _scatter_add(tgt, idx, src, axis=0):
    return tgt.at[idx].add(src)

def _segment_sum(src, seg, n):
    return jax.ops.segment_sum(src, seg, n)
kernel_name = 'mk_prb_d1_jaxref_r4_1e4857'

def setup_inputs(seed: int=0):
    np.random.seed(seed)
    _w = jnp.asarray

    def _L0_attn_setup():
        import jax, jax.numpy as jnp
        import numpy as np
        IN_DIM = 256
        OUT_DIM = 256
        key = jax.random.key(seed)
        ks = jax.random.split(key, 7)
        B, S = (4, 512)
        x = jax.random.normal(ks[0], (B, S, IN_DIM), dtype=jnp.float32)
        s = 1.0 / np.sqrt(IN_DIM)
        Wk = jax.random.uniform(ks[1], (OUT_DIM, IN_DIM), minval=-s, maxval=s, dtype=jnp.float32)
        Wq = jax.random.uniform(ks[2], (OUT_DIM, IN_DIM), minval=-s, maxval=s, dtype=jnp.float32)
        Wv = jax.random.uniform(ks[3], (OUT_DIM, IN_DIM), minval=-s, maxval=s, dtype=jnp.float32)
        bk = jax.random.uniform(ks[4], (OUT_DIM,), minval=-s, maxval=s, dtype=jnp.float32)
        bq = jax.random.uniform(ks[5], (OUT_DIM,), minval=-s, maxval=s, dtype=jnp.float32)
        bv = jax.random.uniform(ks[6], (OUT_DIM,), minval=-s, maxval=s, dtype=jnp.float32)
        return {'x': x, 'Wk': Wk, 'bk': bk, 'Wq': Wq, 'bq': bq, 'Wv': Wv, 'bv': bv}
    _L0_attn_in = _L0_attn_setup()

    def _L0_ffn_setup():
        import jax, jax.numpy as jnp
        import numpy as np
        DIM = 256

        def _reference_tuple_inner(x, W_r, W_k, W_v, mu_r, mu_k):
            B, T, C = x.shape
            x_prev = jnp.concatenate([jnp.zeros((B, 1, C), x.dtype), x[:, :-1, :]], axis=1)
            xr = mu_r * x + (1.0 - mu_r) * x_prev
            xk = mu_k * x + (1.0 - mu_k) * x_prev
            r = jax.nn.sigmoid(jnp.einsum('btc,dc->btd', xr, W_r))
            k = jnp.einsum('btc,dc->btd', xk, W_k)
            k_act = jnp.square(jax.nn.relu(k))
            out = r * jnp.einsum('btc,dc->btd', k_act, W_v)
            new_state = x[:, -1, :]
            return (out, new_state)
        key = jax.random.key(seed)
        ks = jax.random.split(key, 6)
        B, T, C = (8, 512, DIM)
        x = jax.random.normal(ks[0], (B, T, C), dtype=jnp.float32)
        s = 1.0 / np.sqrt(C)
        W_r = jax.random.uniform(ks[1], (C, C), jnp.float32, -s, s)
        W_k = jax.random.uniform(ks[2], (C, C), jnp.float32, -s, s)
        W_v = jax.random.uniform(ks[3], (C, C), jnp.float32, -s, s)
        mu_r = jax.random.uniform(ks[4], (C,), jnp.float32)
        mu_k = jax.random.uniform(ks[5], (C,), jnp.float32)
        return {'x': x, 'W_r': W_r, 'W_k': W_k, 'W_v': W_v, 'mu_r': mu_r, 'mu_k': mu_k}
    _L0_ffn_in = _L0_ffn_setup()
    _d = {'L0_attn_x': _L0_attn_in['x'], 'L0_attn_Wk': _L0_attn_in['Wk'], 'L0_attn_bk': _L0_attn_in['bk'], 'L0_attn_Wq': _L0_attn_in['Wq'], 'L0_attn_bq': _L0_attn_in['bq'], 'L0_attn_Wv': _L0_attn_in['Wv'], 'L0_attn_bv': _L0_attn_in['bv'], 'L0_ffn_W_r': _L0_ffn_in['W_r'], 'L0_ffn_W_k': _L0_ffn_in['W_k'], 'L0_ffn_W_v': _L0_ffn_in['W_v'], 'L0_ffn_mu_r': _L0_ffn_in['mu_r'], 'L0_ffn_mu_k': _L0_ffn_in['mu_k']}
    _x0 = _d['L0_attn_x']
    _d['L0_attn_x'] = jax.random.normal(jax.random.fold_in(jax.random.key(seed), 1), (16, 512, 256), dtype=_x0.dtype)
    del _x0
    return _d

def reference(L0_attn_x, L0_attn_Wk, L0_attn_bk, L0_attn_Wq, L0_attn_bq, L0_attn_Wv, L0_attn_bv, L0_ffn_W_r, L0_ffn_W_k, L0_ffn_W_v, L0_ffn_mu_r, L0_ffn_mu_k):

    def _L0_attn_ref(x, Wk, bk, Wq, bq, Wv, bv):
        import jax, jax.numpy as jnp
        import numpy as np
        IN_DIM = 256
        OUT_DIM = 256
        k = jnp.einsum('bsi,oi->bso', x, Wk) + bk
        q = jnp.einsum('bsi,oi->bso', x, Wq) + bq
        v = jnp.einsum('bsi,oi->bso', x, Wv) + bv
        d = k.shape[-1]
        scores = jnp.einsum('bqd,bkd->bqk', q, k) * d ** (-0.5)
        S = x.shape[1]
        causal = jnp.tril(jnp.ones((S, S), dtype=bool))
        scores = jnp.where(causal, scores, -jnp.inf)
        attn = jax.nn.softmax(scores, axis=-1)
        return jnp.einsum('bqk,bkd->bqd', attn, v)

    def _L0_ffn_ref(x, W_r, W_k, W_v, mu_r, mu_k):
        import jax, jax.numpy as jnp
        import numpy as np
        DIM = 256

        def _reference_tuple_inner(x, W_r, W_k, W_v, mu_r, mu_k):
            B, T, C = x.shape
            x_prev = jnp.concatenate([jnp.zeros((B, 1, C), x.dtype), x[:, :-1, :]], axis=1)
            xr = mu_r * x + (1.0 - mu_r) * x_prev
            xk = mu_k * x + (1.0 - mu_k) * x_prev
            r = jax.nn.sigmoid(jnp.einsum('btc,dc->btd', xr, W_r))
            k = jnp.einsum('btc,dc->btd', xk, W_k)
            k_act = jnp.square(jax.nn.relu(k))
            out = r * jnp.einsum('btc,dc->btd', k_act, W_v)
            new_state = x[:, -1, :]
            return (out, new_state)
        return _reference_tuple_inner(x, W_r, W_k, W_v, mu_r, mu_k)[0]
    x = L0_attn_x
    xn = _layernorm(x, axis=-1)
    x = x + _L0_attn_ref(xn, L0_attn_Wk, L0_attn_bk, L0_attn_Wq, L0_attn_bq, L0_attn_Wv, L0_attn_bv) + _L0_ffn_ref(xn, L0_ffn_W_r, L0_ffn_W_k, L0_ffn_W_v, L0_ffn_mu_r, L0_ffn_mu_k)
    return x

_drawn_inputs = setup_inputs


def setup_inputs(seed=0):
    import zlib

    import numpy as np

    out = dict(_drawn_inputs(seed))
    spreads = {}
    factors = {'L0_attn_bk': 64.0, 'L0_attn_bq': 37.212, 'L0_ffn_W_r': 3.182, 'L0_ffn_mu_r': 6.403}
    for name, (base, spread) in spreads.items():
        noise = np.random.default_rng([zlib.crc32(name.encode()), seed]).standard_normal(out[name].shape)
        drawn = base * np.exp(spread * noise) if base else spread * noise
        out[name] = jnp.asarray(drawn.astype(out[name].dtype))
    for name, factor in factors.items():
        out[name] = (out[name] * factor).astype(out[name].dtype)
    return out
```

```python
import concourse.bass as bass
from concourse import mybir
from contextlib import ExitStack


def attention_and_channel_mix_kernel(nc, x, Wk, bk, Wq, bq, Wv, bv, Wr, Wkf, Wvf, mu_r, mu_k, out):
    F32 = mybir.dt.float32
    F32R = mybir.dt.float32r
    BF16 = mybir.dt.bfloat16
    ALU = mybir.AluOpType
    ACT = mybir.ActivationFunctionType
    AX = mybir.AxisListType

    B, S, D = x.shape
    P = 128
    NT = S // P
    NC = D // P
    EPS = 1e-5
    UNIT = float(D) ** -0.5
    MASKED = -1e30
    PAIR = 2 * D
    LOOP = (1, B - 2)

    PROB_AT = {3: 0, 2: 512, 0: 896, 1: 1024}
    PROB_COLS = 1280
    PROB_GROUPS = ((0, 512), (512, 1024), (1024, 1280))
    PROB_TILES = ((3,), (2, 0), (1,))
    SCORES = {3: (0, 0), 2: (1, 0), 1: (2, 0), 0: (2, 256)}
    SCORE_ORDER = (3, 2, 1, 0)
    XT_BANK = (3, 4)
    T_BANK = (5, 4)
    KEY_BANK = (5, 6)
    PROB_BANK = (7, 0, 1)
    GATE_BANK = (2, 3)
    ATTN_BANK = (4, 5)
    FFN_BANK = (6, 7)
    V_BANK = (6, 7)

    ctx = ExitStack()
    with ctx:
        def sb(name, shape, dt=F32):
            return ctx.enter_context(nc.sbuf_tensor(name, shape, dt))

        def sem(name):
            return ctx.enter_context(nc.semaphore(name))

        x_all = sb("x_all", [P, B, NT, D])
        xn = sb("xn", [P, NT, D])
        xT = sb("xT", [P, NC, S + 2])
        x_hi, x_lo = sb("x_hi", [P, NC, S], F32R), sb("x_lo", [P, NC, S], F32R)
        diff = sb("diff", [P, NC, S])
        mixk, mixr = sb("mixk", [P, NC, S]), sb("mixr", [P, NC, S])
        mixk_hi, mixk_lo = sb("mixk_hi", [P, NC, S], F32R), sb("mixk_lo", [P, NC, S], F32R)
        mixr_hi, mixr_lo = sb("mixr_hi", [P, NC, S], F32R), sb("mixr_lo", [P, NC, S], F32R)
        t_hi, t_lo = sb("t_hi", [P, NC, S], F32R), sb("t_lo", [P, NC, S], F32R)
        v_hi, v_lo = sb("v_hi", [P, NT, D], F32R), sb("v_lo", [P, NT, D], F32R)
        probs = sb("probs", [P, PROB_COLS])
        pT_hi, pT_lo = sb("pT_hi", [P, PROB_COLS], F32R), sb("pT_lo", [P, PROB_COLS], F32R)
        relu = sb("relu", [P, NC, S])
        act = sb("act", [P, NC, S])
        act_hi, act_lo = sb("act_hi", [P, NC, S], F32R), sb("act_lo", [P, NC, S], F32R)
        gate = sb("gate", [P, NT, D])
        attn = sb("attn", [P, NT, D])
        ffn = sb("ffn", [P, NT, D])
        y = sb("y", [P, NT, D])
        stats = sb("stats", [P, NT, 6])
        mv = sb("mv", [P, NT, 2])
        var_eps, rstd = sb("var_eps", [P, NT]), sb("rstd", [P, NT])
        neg_half = sb("neg_half", [P, NT])
        neg_max, row_sum, inv_sum = sb("neg_max", [P, NT]), sb("row_sum", [P, NT]), sb("inv_sum", [P, NT])
        ident = sb("ident", [P, P])
        ident_b, mask_b = sb("ident_b", [P, P], BF16), sb("mask_b", [P, P], BF16)
        raw = {n: sb(f"raw_{n}", [P, NC, D]) for n in ("q", "k", "v", "r", "kf", "vf")}
        bias = {n: sb(f"bias_{n}", [P, NC]) for n in ("q", "k", "v")}
        row_total = {n: sb(f"row_total_{n}", [P, NC]) for n in ("q", "k", "v")}
        shift = {n: sb(f"shift_{n}", [P, NC]) for n in ("q", "k", "v")}
        mu = {n: sb(f"mu_{n}", [P, NC]) for n in ("r", "k")}
        w_hi = {n: sb(f"w_hi_{n}", [P, NC, D], F32R) for n in ("m", "v", "kf", "r", "vf")}
        w_lo = {n: sb(f"w_lo_{n}", [P, NC, D], F32R) for n in ("m", "v", "kf", "r", "vf")}

        psum = ctx.enter_context(nc.psum_tensor("psum", [P, 8, 512], F32))

        def tile_of(banks, i):
            return psum[:, banks[i // 2], (i % 2) * D:(i % 2 + 1) * D]

        def score_tile(i, cols):
            bank, at = SCORES[i]
            return psum[:, bank, at:at + cols]

        def f32(ap):
            return ap.bitcast(F32)

        x_loaded = sem("x_loaded")
        x0_loaded = sem("x0_loaded")
        y_stored = sem("y_stored")
        qk_loaded, v_loaded, ffn_w_loaded = sem("qk_loaded"), sem("v_loaded"), sem("ffn_w_loaded")
        mu_loaded = sem("mu_loaded")
        consts_ready, zeroed = sem("consts_ready"), sem("zeroed")
        stats_ready, mv_ready = sem("stats_ready"), sem("mv_ready")
        var_ready, rstd_ready = sem("var_ready"), sem("rstd_ready")
        xn_ready = sem("xn_ready")
        xT_ready = sem("xT_ready")
        xT_copied, x_hi_ready, x_lo_ready = sem("xT_copied"), sem("x_hi_ready"), sem("x_lo_ready")
        diff_ready = sem("diff_ready")
        mixk_ready, mixk_hi_ready, mixk_lo_ready = sem("mixk_ready"), sem("mixk_hi_ready"), sem("mixk_lo_ready")
        mixr_ready, mixr_hi_ready, mixr_lo_ready = sem("mixr_ready"), sem("mixr_hi_ready"), sem("mixr_lo_ready")
        t_ready, t_hi_ready, t_lo_ready = sem("t_ready"), sem("t_hi_ready"), sem("t_lo_ready")
        v_ready, v_hi_ready, v_lo_ready = sem("v_ready"), sem("v_hi_ready"), sem("v_lo_ready")
        scores_ready, max_ready, exp_ready = sem("scores_ready"), sem("max_ready"), sem("exp_ready")
        pT_ready, pT_hi_ready, pT_lo_ready = sem("pT_ready"), sem("pT_hi_ready"), sem("pT_lo_ready")
        inv_ready = sem("inv_ready")
        attn_ready, attn_added = sem("attn_ready"), sem("attn_added")
        key_ready, relu_ready = sem("key_ready"), sem("relu_ready")
        act_ready, act_hi_ready, act_lo_ready = sem("act_ready"), sem("act_hi_ready"), sem("act_lo_ready")
        gate_ready, tanh_ready = sem("gate_ready"), sem("tanh_ready")
        ffn_ready, ffn_gated = sem("ffn_ready"), sem("ffn_gated")
        y_ready = sem("y_ready")
        total_ready, mean_ready, shift_ready = sem("total_ready"), sem("mean_ready"), sem("shift_ready")
        qk_shifted, v_shifted = sem("qk_shifted"), sem("v_shifted")
        w_ready, w_hi_ready, w_lo_ready = sem("w_ready"), sem("w_hi_ready"), sem("w_lo_ready")

        W_ORDER = (("m", 5), ("v", 6), ("kf", 0), ("r", 1), ("vf", 2))
        W_SCALE = {"m": 1.0, "v": 1.0, "kf": 1.0, "r": 1.0, "vf": 0.5}
        W_AT = {n: i + 1 for i, (n, _) in enumerate(W_ORDER)}

        block = ctx.enter_context(nc.Block())

        x_v = x.rearrange("b (t p) d -> b p t d", p=P)
        out_v = out.rearrange("b (t p) d -> b p t d", p=P)

        @block.sync
        def _(sp):
            for t in range(NT):
                sp.dma_start(x_all[:, 0, t, :], x_v[0, :, t, :]).then_inc(x0_loaded, 16)
            sp.dma_start(x_all[:, 1, :, :], x_v[1]).then_inc(x_loaded, 16)

            def turn(b, load, halves=1):
                if load:
                    sp.wait_ge(x_loaded, 16 * b + 16)
                    sp.dma_start(x_all[:, b + 2, :, :], x_v[b + 2]).then_inc(x_loaded, 16)
                k = NT // halves
                for h in range(halves):
                    sp.wait_ge(y_ready, 2 * b + 2 - (halves - 1 - h))
                    sp.dma_start(out_v[b, :, h * k:(h + 1) * k, :], y[:, h * k:(h + 1) * k, :]).then_inc(y_stored, 16)

            turn(0, load=True)
            with sp.Fori(*LOOP) as b:
                turn(b, load=True)
            turn(B - 2, load=False)
            turn(B - 1, load=False, halves=2)
            sp.wait_ge(y_stored, 16 * (B + 1))

        @block.tensor
        def _(pe):
            def three_passes(dst, parts, extra=None):
                ops = []
                for (s_hi, s_lo), (m_hi, m_lo) in parts:
                    ops += [(s_hi, m_hi), (s_hi, m_lo), (s_lo, m_hi)]
                for n, (s, m) in enumerate(ops):
                    last = nc.tensor.matmul(dst, s, m, start=(n == 0), stop=(n == len(ops) - 1))
                    if n == 0 and extra:
                        extra()
                return last

            def halves(hi, lo, c, cols):
                return hi[:, c, cols], lo[:, c, cols]

            def transpose_x(b, first=False):
                pe.wait_ge(xn_ready, 4 * b + 4)
                if not first:
                    pe.wait_ge(tanh_ready, 2 * b - 2)
                for c in range(NC):
                    for i in range(NT):
                        last = nc.tensor.transpose(psum[:, XT_BANK[c], i * P:(i + 1) * P],
                                                   xn[:, i, c * P:(c + 1) * P], ident[:, :])
                    last.then_inc(xT_ready, 1)

            def project_t(b, first=False):
                pe.wait_ge(x_lo_ready, b + 1)
                pe.wait_ge(x_hi_ready, 2 * b + 2)
                for d in range(NC):
                    if not first:
                        pe.wait_ge(attn_added, 4 * b - 2 + 2 * d)
                    three_passes(psum[:, T_BANK[d], :], [
                        (halves(w_hi["m"], w_lo["m"], c, slice(d * P, (d + 1) * P)), halves(x_hi, x_lo, c, slice(0, S)))
                        for c in range(NC)]).then_inc(t_ready, 1)

            def project_v(b, first=False):
                for i in range(NT):
                    if i % 2 == 0 and not first:
                        pe.wait_ge(ffn_gated, 2 * b - 1 + i // 2)
                    last = three_passes(tile_of(V_BANK, i), [
                        (halves(x_hi, x_lo, c, slice(i * P, (i + 1) * P)), halves(w_hi["v"], w_lo["v"], c, slice(0, D)))
                        for c in range(NC)])
                    if i % 2 == 1:
                        last.then_inc(v_ready, 1)

            pe.wait_ge(consts_ready, 5)
            transpose_x(0, first=True)
            pe.wait_ge(qk_shifted, 4)
            for c in range(NC):
                for o in range(NC):
                    last = nc.tensor.matmul(psum[:, 5, c * D:(c + 1) * D], raw["k"][:, o, c * P:(c + 1) * P],
                                            raw["q"][:, o, :], start=(o == 0), stop=(o == NC - 1))
            last.then_inc(w_ready, 1)
            for n, bank in W_ORDER[1:]:
                if n == "v":
                    pe.wait_ge(v_shifted, 2)
                if n == "kf":
                    pe.wait_ge(ffn_w_loaded, 48)
                for c in range(NC):
                    for o in range(NC):
                        last = nc.tensor.transpose(psum[:, bank, c * D + o * P:c * D + (o + 1) * P],
                                                   raw[n][:, o, c * P:(c + 1) * P], ident[:, :])
                last.then_inc(w_ready, 1)
                if n == "v":
                    pe.wait_ge(w_lo_ready, W_AT["m"])
                    project_t(0, first=True)
                    pe.wait_ge(w_lo_ready, W_AT["v"])
                    project_v(0, first=True)
            pe.wait_ge(w_lo_ready, len(W_ORDER))

            def turn(b, following):
                pe.wait_ge(t_lo_ready, 2 * b + 2)
                for i in SCORE_ORDER:
                    if i == 1:
                        pe.wait_ge(tanh_ready, 2 * b)
                    cols = max((i + 1) * P, 256)
                    def mask():
                        nc.tensor.matmul(psum[:, SCORES[i][0], SCORES[i][1] + i * P:SCORES[i][1] + (i + 1) * P],
                                         ident_b[:, :], mask_b[:, :], start=False, stop=False)
                    three_passes(score_tile(i, cols), [
                        (halves(x_hi, x_lo, c, slice(i * P, (i + 1) * P)), halves(t_hi, t_lo, c, slice(0, cols)))
                        for c in range(NC)], extra=mask).then_inc(scores_ready, 1)
                if following:
                    transpose_x(b + 1)
                pe.wait_ge(mixk_lo_ready, b + 1)
                pe.wait_ge(v_lo_ready, 2 * b + 1)
                for o in range(NC):
                    three_passes(psum[:, KEY_BANK[o], :], [
                        (halves(w_hi["kf"], w_lo["kf"], c, slice(o * P, (o + 1) * P)), halves(mixk_hi, mixk_lo, c, slice(0, S)))
                        for c in range(NC)]).then_inc(key_ready, 1)
                pe.wait_ge(v_lo_ready, 2 * b + 2)
                for g, tiles in enumerate(PROB_TILES):
                    if g == 0:
                        pe.wait_ge(exp_ready, 4 * b + 1)
                    if g == 1:
                        pe.wait_ge(exp_ready, 4 * b + 4)
                    for i in tiles:
                        for j in range(i + 1):
                            at = PROB_AT[i] + j * P
                            last = nc.tensor.transpose(psum[:, PROB_BANK[g], at % 512:at % 512 + P],
                                                       probs[:, at:at + P], ident[:, :])
                    last.then_inc(pT_ready, 1)
                pe.wait_ge(mixr_lo_ready, b + 1)
                if following:
                    pe.wait_ge(x_hi_ready, 2 * b + 4)
                for i in range(NT):
                    last = three_passes(tile_of(GATE_BANK, i), [
                        (halves(mixr_hi, mixr_lo, c, slice(i * P, (i + 1) * P)), halves(w_hi["r"], w_lo["r"], c, slice(0, D)))
                        for c in range(NC)])
                    if i % 2 == 1:
                        last.then_inc(gate_ready, 1)
                pe.wait_ge(pT_lo_ready, 3 * b + 3)
                pe.wait_ge(relu_ready, 2 * b + 2)
                for i in (3, 2, 1, 0):
                    last = three_passes(tile_of(ATTN_BANK, i), [
                        ((pT_hi[:, PROB_AT[i] + j * P:PROB_AT[i] + (j + 1) * P], pT_lo[:, PROB_AT[i] + j * P:PROB_AT[i] + (j + 1) * P]),
                         (v_hi[:, j, :], v_lo[:, j, :])) for j in range(i + 1)])
                    if i % 2 == 0:
                        last.then_inc(attn_ready, 1)
                pe.wait_ge(act_lo_ready, 2 * b + 2)
                for i in range(NT):
                    last = three_passes(tile_of(FFN_BANK, i), [
                        (halves(act_hi, act_lo, c, slice(i * P, (i + 1) * P)), halves(w_hi["vf"], w_lo["vf"], c, slice(0, D)))
                        for c in range(NC)])
                    if i % 2 == 1:
                        last.then_inc(ffn_ready, 1)
                if following:
                    project_t(b + 1)
                    project_v(b + 1)

            turn(0, True)
            with pe.Fori(*LOOP) as b:
                turn(b, True)
            turn(B - 2, True)
            turn(B - 1, False)

        @block.scalar
        def _(sc):
            for n, w_in, b_in in (("q", Wq, bq), ("k", Wk, bk)):
                sc.dma_start(raw[n][:, :, :], w_in.rearrange("(o p) c -> p o c", p=P)).then_inc(qk_loaded, 16)
                sc.dma_start(bias[n][:, :], b_in.rearrange("(o p) -> p o", p=P), allow_slow_non_contiguous=True).then_inc(qk_loaded, 16)
            sc.dma_start(raw["v"][:, :, :], Wv.rearrange("(o p) c -> p o c", p=P)).then_inc(v_loaded, 16)
            sc.dma_start(bias["v"][:, :], bv.rearrange("(o p) -> p o", p=P), allow_slow_non_contiguous=True).then_inc(v_loaded, 16)
            for n, m_in in (("k", mu_k), ("r", mu_r)):
                sc.dma_start(mu[n][:, :], m_in.rearrange("(c p) -> p c", p=P), allow_slow_non_contiguous=True).then_inc(mu_loaded, 16)
            for n, w_in in (("kf", Wkf), ("r", Wr), ("vf", Wvf)):
                sc.dma_start(raw[n][:, :, :], w_in.rearrange("(o p) c -> p o c", p=P)).then_inc(ffn_w_loaded, 16)

            def copy_x(b):
                sc.wait_ge(mixr_ready, b)
                for c in range(NC):
                    sc.wait_ge(xT_ready, 2 * b + c + 1)
                    nc.scalar.activation(xT[:, c, 1:S + 1], psum[:, XT_BANK[c], :], ACT.Copy).then_inc(xT_copied, 1)
                    nc.scalar.activation(x_hi[:, c, :], psum[:, XT_BANK[c], :], ACT.Copy, bias=UNIT).then_inc(x_hi_ready, 1)

            def upper_mix(b, src, dst, src_ready, dst_ready, read):
                sc.wait_ge(src_ready, b + 1)
                sc.wait_ge(read, 2 * b)
                nc.scalar.activation(dst[:, :, :], src[:, :, :], ACT.Copy).then_inc(dst_ready, 1)

            def upper_t(b):
                for d in range(NC):
                    sc.wait_ge(t_ready, 2 * b + d + 1)
                    nc.scalar.activation(t_hi[:, d, :], psum[:, T_BANK[d], :], ACT.Copy).then_inc(t_hi_ready, 1)

            def upper_v(b):
                for h in range(2):
                    sc.wait_ge(v_ready, 2 * b + h + 1)
                    nc.scalar.activation(v_hi[:, 2 * h:2 * h + 2, :], psum[:, V_BANK[h], :].rearrange("p (t d) -> p t d", d=D),
                                         ACT.Copy).then_inc(v_hi_ready, 1)

            def upper_w(n, bank):
                sc.wait_ge(w_ready, W_AT[n])
                nc.scalar.activation(w_hi[n][:, :, :], psum[:, bank, :].rearrange("p (c o) -> p c o", o=D),
                                     ACT.Copy, scale=W_SCALE[n]).then_inc(w_hi_ready, 1)

            copy_x(0)
            for n, bank in W_ORDER[:2]:
                upper_w(n, bank)
            upper_t(0)
            upper_v(0)
            for n, bank in W_ORDER[2:]:
                upper_w(n, bank)
            upper_mix(0, mixk, mixk_hi, mixk_ready, mixk_hi_ready, key_ready)
            upper_mix(0, mixr, mixr_hi, mixr_ready, mixr_hi_ready, gate_ready)

            def turn(b, following):
                for n, i in enumerate(SCORE_ORDER):
                    sc.wait_ge(max_ready, 3 * b + min(n, 2) + 1)
                    nc.scalar.activation(probs[:, PROB_AT[i]:PROB_AT[i] + (i + 1) * P], score_tile(i, (i + 1) * P), ACT.Exp,
                                         bias=neg_max[:, i:i + 1], accum_out=row_sum[:, i:i + 1]).then_inc(exp_ready, 1)
                if following:
                    copy_x(b + 1)
                sc.wait_ge(act_ready, 2 * b)
                for o in range(NC):
                    sc.wait_ge(key_ready, 2 * b + o + 1)
                    nc.scalar.activation(relu[:, o, :], psum[:, KEY_BANK[o], :], ACT.Relu).then_inc(relu_ready, 1)
                for g, (lo, hi) in enumerate(PROB_GROUPS):
                    sc.wait_ge(pT_ready, 3 * b + g + 1)
                    nc.scalar.activation(pT_hi[:, lo:hi], psum[:, PROB_BANK[g], 0:hi - lo], ACT.Copy).then_inc(pT_hi_ready, 1)
                for o in range(NC):
                    sc.wait_ge(act_ready, 2 * b + o + 1)
                    nc.scalar.activation(act_hi[:, o, :], act[:, o, :], ACT.Copy).then_inc(act_hi_ready, 1)
                sc.wait_ge(ffn_gated, 2 * b)
                for h in range(2):
                    sc.wait_ge(gate_ready, 2 * b + h + 1)
                    nc.scalar.activation(gate[:, 2 * h:2 * h + 2, :], psum[:, GATE_BANK[h], :].rearrange("p (t d) -> p t d", d=D),
                                         ACT.Tanh, scale=0.5).then_inc(tanh_ready, 1)
                if following:
                    upper_mix(b + 1, mixk, mixk_hi, mixk_ready, mixk_hi_ready, key_ready)
                    upper_mix(b + 1, mixr, mixr_hi, mixr_ready, mixr_hi_ready, gate_ready)
                    upper_t(b + 1)
                    upper_v(b + 1)

            turn(0, True)
            with sc.Fori(*LOOP) as b:
                turn(b, True)
            turn(B - 2, True)
            turn(B - 1, False)

        @block.vector
        def _(dv):
            def statistics(b, loaded):
                for t in range(NT):
                    loaded(t)
                    nc.vector.bn_stats(stats[:, t, :], x_all[:, b, t, :]).then_inc(stats_ready, 1)

            def aggregate(b):
                for t in range(NT):
                    nc.vector.bn_aggr(mv[:, t, :], stats[:, t, :]).then_inc(mv_ready, 1)
                dv.wait_ge(mv_ready, 4 * b + 4)
                nc.vector.tensor_scalar(var_eps[:, :], mv[:, :, 1], EPS, None, ALU.add).then_inc(var_ready, 1)

            def normalise(b):
                dv.wait_ge(rstd_ready, b + 1)
                dv.wait_ge(xT_ready, 2 * b)
                for t in range(NT):
                    nc.vector.tensor_scalar(xn[:, t, :], x_all[:, b, t, :], mv[:, t, 0:1], rstd[:, t:t + 1],
                                            ALU.subtract, ALU.mult).then_inc(xn_ready, 1)

            def lower_x(b):
                dv.wait_ge(x_hi_ready, 2 * b + 2)
                nc.vector.scalar_tensor_tensor(out=x_lo[:, :, :], in0=xT[:, :, 1:S + 1], scalar=UNIT, in1=f32(x_hi[:, :, :]),
                                               op0=ALU.add, op1=ALU.subtract).then_inc(x_lo_ready, 1)

            def mix(b, m, dst, ready, lo_ready):
                dv.wait_ge(diff_ready, b + 1)
                dv.wait_ge(lo_ready, b)
                for c in range(NC):
                    last = nc.vector.scalar_tensor_tensor(out=dst[:, c, :], in0=diff[:, c, :], scalar=mu[m][:, c:c + 1],
                                                          in1=xT[:, c, 0:S], op0=ALU.mult, op1=ALU.add)
                last.then_inc(ready, 1)

            def lower_t(b):
                for d in range(NC):
                    dv.wait_ge(t_hi_ready, 2 * b + d + 1)
                    nc.vector.tensor_tensor(t_lo[:, d, :], psum[:, T_BANK[d], :], f32(t_hi[:, d, :]),
                                            ALU.subtract).then_inc(t_lo_ready, 1)

            def lower_v(b):
                for h in range(2):
                    dv.wait_ge(v_hi_ready, 2 * b + h + 1)
                    nc.vector.tensor_tensor(v_lo[:, 2 * h:2 * h + 2, :], psum[:, V_BANK[h], :].rearrange("p (t d) -> p t d", d=D),
                                            f32(v_hi[:, 2 * h:2 * h + 2, :]), ALU.subtract).then_inc(v_lo_ready, 1)

            def lower_w(n, bank):
                dv.wait_ge(w_hi_ready, W_AT[n])
                nc.vector.scalar_tensor_tensor(out=w_lo[n][:, :, :], in0=psum[:, bank, :].rearrange("p (c o) -> p c o", o=D),
                                               scalar=W_SCALE[n], in1=f32(w_hi[n][:, :, :]), op0=ALU.mult,
                                               op1=ALU.subtract).then_inc(w_lo_ready, 1)

            def prepare(n, loaded, at, count, ready, scale):
                dv.wait_ge(loaded, count)
                nc.vector.tensor_reduce(row_total[n][:, :], raw[n][:, :, :], AX.X, ALU.add).then_inc(total_ready, 1)
                dv.wait_ge(total_ready, at)
                nc.vector.tensor_scalar(row_total[n][:, :], row_total[n][:, :], -1.0 / D, None, ALU.mult).then_inc(mean_ready, 1)
                dv.wait_ge(mean_ready, at)
                nc.vector.scalar_tensor_tensor(out=shift[n][:, :], in0=bias[n][:, :], scalar=UNIT, in1=row_total[n][:, :],
                                               op0=ALU.mult, op1=ALU.add).then_inc(shift_ready, 1)
                dv.wait_ge(shift_ready, at)
                for o in range(NC):
                    nc.vector.tensor_scalar(raw[n][:, o, :], raw[n][:, o, :], shift[n][:, o:o + 1], scale,
                                            ALU.add, ALU.mult).then_inc(ready, 1)

            statistics(0, lambda t: dv.wait_ge(x0_loaded, 16 * NT))
            dv.wait_ge(stats_ready, 4)
            aggregate(0)
            prepare("q", qk_loaded, 1, 64, qk_shifted, UNIT)
            prepare("k", qk_loaded, 2, 64, qk_shifted, 1.0)
            normalise(0)
            prepare("v", v_loaded, 3, 32, v_shifted, 1.0)
            lower_x(0)
            for n, bank in W_ORDER[:2]:
                lower_w(n, bank)
            lower_t(0)
            statistics(1, lambda t: dv.wait_ge(x_loaded, 16))
            dv.wait_ge(stats_ready, 8)
            aggregate(1)
            lower_v(0)
            normalise(1)
            dv.wait_ge(mu_loaded, 32)
            mix(0, "k", mixk, mixk_ready, mixk_lo_ready)
            mix(0, "r", mixr, mixr_ready, mixr_lo_ready)
            for n, bank in W_ORDER[2:]:
                lower_w(n, bank)

            def turn(b, following, after_next):
                for n, i in enumerate(SCORE_ORDER):
                    if i > 0:
                        dv.wait_ge(scores_ready, 4 * b + (n + 1 if i > 1 else 4))
                    last = nc.vector.tensor_reduce(neg_max[:, i:i + 1], score_tile(i, (i + 1) * P), AX.X, ALU.max,
                                                   negate=True)
                    if i != 1:
                        last.then_inc(max_ready, 1)
                if after_next:
                    statistics(b + 2, lambda t: dv.wait_ge(x_loaded, 16 * b + 32) if t == 0 else None)
                    dv.wait_ge(stats_ready, 4 * b + 12)
                if following:
                    lower_x(b + 1)
                if after_next:
                    aggregate(b + 2)
                for g, (lo, hi) in enumerate(PROB_GROUPS):
                    dv.wait_ge(pT_hi_ready, 3 * b + g + 1)
                    nc.vector.tensor_tensor(pT_lo[:, lo:hi], psum[:, PROB_BANK[g], 0:hi - lo], f32(pT_hi[:, lo:hi]),
                                            ALU.subtract).then_inc(pT_lo_ready, 1)
                if following:
                    mix(b + 1, "k", mixk, mixk_ready, mixk_lo_ready)
                    mix(b + 1, "r", mixr, mixr_ready, mixr_lo_ready)
                dv.wait_ge(exp_ready, 4 * b + 4)
                nc.vector.reciprocal(inv_sum[:, :], row_sum[:, :]).then_inc(inv_ready, 1)
                dv.wait_ge(inv_ready, b + 1)
                for n, i in enumerate((3, 2, 1, 0)):
                    dv.wait_ge(attn_ready, 2 * b + n // 2 + 1)
                    nc.vector.scalar_tensor_tensor(out=attn[:, i, :], in0=tile_of(ATTN_BANK, i), scalar=inv_sum[:, i:i + 1],
                                                   in1=x_all[:, b, i, :], op0=ALU.mult, op1=ALU.add).then_inc(attn_added, 1)
                dv.wait_ge(tanh_ready, 2 * b + 2)
                dv.wait_ge(attn_added, 4 * b + 4)
                dv.wait_ge(y_stored, 16 * b)
                for h in range(2):
                    two = slice(2 * h, 2 * h + 2)
                    dv.wait_ge(ffn_ready, 2 * b + h + 1)
                    nc.vector.scalar_tensor_tensor(out=ffn[:, two, :], in0=gate[:, two, :], scalar=1.0,
                                                   in1=psum[:, FFN_BANK[h], :].rearrange("p (t d) -> p t d", d=D),
                                                   op0=ALU.add, op1=ALU.mult).then_inc(ffn_gated, 1)
                    dv.wait_ge(ffn_gated, 2 * b + h + 1)
                    nc.vector.tensor_tensor(y[:, two, :], attn[:, two, :], ffn[:, two, :], ALU.add).then_inc(y_ready, 1)
                if following:
                    lower_t(b + 1)
                if after_next:
                    normalise(b + 2)
                if following:
                    lower_v(b + 1)

            turn(0, True, True)
            with dv.Fori(*LOOP) as b:
                turn(b, True, True)
            turn(B - 2, True, False)
            turn(B - 1, False, False)

        @block.gpsimd
        def _(gp):
            gp.memset(neg_half[:, :], -0.5).then_inc(consts_ready, 1)
            gp.memset(xT[:, :, 0:1], 0.0).then_inc(consts_ready, 1)
            for tile, fill in ((ident, 0.0), (ident_b, 0.0), (mask_b, 0.0)):
                gp.memset(tile[:, :], fill).then_inc(zeroed, 1)
            gp.wait_ge(zeroed, 3)
            for tile in (ident, ident_b):
                gp.affine_select(out=tile[:, :], in_=tile[:, :], compare_op=ALU.not_equal, fill=1.0, base=0,
                                 pattern=[[-1, P]], channel_multiplier=1).then_inc(consts_ready, 1)
            gp.affine_select(out=mask_b[:, :], in_=mask_b[:, :], compare_op=ALU.is_ge, fill=MASKED, base=0,
                             pattern=[[-1, P]], channel_multiplier=1).then_inc(consts_ready, 1)

            def inverse_deviation(b):
                gp.wait_ge(var_ready, b + 1)
                nc.gpsimd.tensor_tensor(rstd[:, :], var_eps[:, :], neg_half[:, :], ALU.pow).then_inc(rstd_ready, 1)

            def difference(b):
                gp.wait_ge(xT_copied, 2 * b + 2)
                gp.wait_ge(mixr_ready, b)
                nc.gpsimd.tensor_tensor(diff[:, :, :], xT[:, :, 1:S + 1], xT[:, :, 0:S], ALU.subtract).then_inc(diff_ready, 1)

            def lower(b, whole, hi, lo, hi_ready, lo_ready):
                gp.wait_ge(hi_ready, b + 1)
                nc.gpsimd.tensor_tensor(lo[:, :, :], whole[:, :, :], f32(hi[:, :, :]), ALU.subtract).then_inc(lo_ready, 1)

            inverse_deviation(0)
            difference(0)
            inverse_deviation(1)
            lower(0, mixk, mixk_hi, mixk_lo, mixk_hi_ready, mixk_lo_ready)
            lower(0, mixr, mixr_hi, mixr_lo, mixr_hi_ready, mixr_lo_ready)

            def turn(b, following, after_next):
                if following:
                    difference(b + 1)
                for o in range(NC):
                    gp.wait_ge(relu_ready, 2 * b + o + 1)
                    if o == 0:
                        gp.wait_ge(act_hi_ready, 2 * b)
                        gp.wait_ge(act_lo_ready, 2 * b)
                    nc.gpsimd.tensor_tensor(act[:, o, :], relu[:, o, :], relu[:, o, :], ALU.mult).then_inc(act_ready, 1)
                for o in range(NC):
                    gp.wait_ge(act_hi_ready, 2 * b + o + 1)
                    nc.gpsimd.tensor_tensor(act_lo[:, o, :], act[:, o, :], f32(act_hi[:, o, :]),
                                            ALU.subtract).then_inc(act_lo_ready, 1)
                if following:
                    lower(b + 1, mixk, mixk_hi, mixk_lo, mixk_hi_ready, mixk_lo_ready)
                if after_next:
                    inverse_deviation(b + 2)
                if following:
                    lower(b + 1, mixr, mixr_hi, mixr_lo, mixr_hi_ready, mixr_lo_ready)

            turn(0, True, True)
            with gp.Fori(*LOOP) as b:
                turn(b, True, True)
            turn(B - 2, True, False)
            turn(B - 1, False, False)


_INS = ["L0_attn_x", "L0_attn_Wk", "L0_attn_bk", "L0_attn_Wq", "L0_attn_bq", "L0_attn_Wv", "L0_attn_bv",
        "L0_ffn_W_r", "L0_ffn_W_k", "L0_ffn_W_v", "L0_ffn_mu_r", "L0_ffn_mu_k"]


def kernel(**inputs):
    import numpy as _np
    import concourse.bacc as _bacc
    from concourse import mybir as _mybir
    from concourse.bass_utils import run_bass_kernel_spmd as _run

    nc = _bacc.Bacc("TRN2", target_bir_lowering=False, num_devices=1)
    arrays, args = {}, []
    for name in _INS:
        a = _np.ascontiguousarray(inputs[name])
        arrays[f"in_{name}"] = a
        args.append(nc.dram_tensor(f"in_{name}", a.shape, _mybir.dt.from_np(a.dtype), kind="ExternalInput").ap())
    out = nc.dram_tensor("out_0", inputs["L0_attn_x"].shape, _mybir.dt.float32, kind="ExternalOutput").ap()
    attention_and_channel_mix_kernel(nc, *args, out)
    r = _run(nc, [arrays], core_ids=[0])
    return r.results[0]["out_0"]
```

```python
import concourse.bass as bass
from concourse import mybir
from contextlib import ExitStack


def attention_and_channel_mix_kernel(nc, x, Wk, bk, Wq, bq, Wv, bv, Wr, Wkf, Wvf, mu_r, mu_k, out):
    F32 = mybir.dt.float32
    F32R = mybir.dt.float32r
    ALU = mybir.AluOpType
    ACT = mybir.ActivationFunctionType
    AX = mybir.AxisListType

    B, S, D = x.shape
    P = 128
    NT = S // P
    NC = D // P
    EPS = 1e-5
    UNIT = float(D) ** -0.5
    MASKED = -1e30
    PAIR = 2 * D
    WARM_UP = 6
    LOOP = (1, B - 2)

    PROB_AT = {3: 0, 2: 512, 0: 896, 1: 1024}
    PROB_COLS = 1280
    PROB_GROUPS = ((0, 512), (512, 1024), (1024, 1280))
    PROB_TILES = ((3,), (2, 0), (1,))
    SCORES = {3: (0, 0), 2: (1, 0), 1: (2, 0), 0: (2, 256)}
    SCORE_ORDER = (3, 2, 1, 0)
    XT_BANK = (3, 4)
    T_BANK = (5, 4)
    KEY_BANK = (5, 6)
    PROB_BANK = (7, 0, 1)
    GATE_BANK = (2, 3)
    ATTN_BANK = (4, 5)
    FFN_BANK = (6, 7)
    V_BANK = (6, 7)

    ctx = ExitStack()
    with ctx:
        def sb(name, shape, dt=F32):
            return ctx.enter_context(nc.sbuf_tensor(name, shape, dt))

        def sem(name):
            return ctx.enter_context(nc.semaphore(name))

        x_all = sb("x_all", [P, B, NT, D])
        xn = sb("xn", [P, NT, D])
        xT = sb("xT", [P, NC, S + 2])
        x_hi, x_lo = sb("x_hi", [P, NC, S], F32R), sb("x_lo", [P, NC, S], F32R)
        x_first, t_first = sb("x_first", [P, NC, P]), sb("t_first", [P, NC, P])
        diff = sb("diff", [P, NC, S])
        mixk, mixr = sb("mixk", [P, NC, S]), sb("mixr", [P, NC, S])
        mixk_hi, mixk_lo = sb("mixk_hi", [P, NC, S], F32R), sb("mixk_lo", [P, NC, S], F32R)
        mixr_hi, mixr_lo = sb("mixr_hi", [P, NC, S], F32R), sb("mixr_lo", [P, NC, S], F32R)
        t_hi, t_lo = sb("t_hi", [P, NC, S], F32R), sb("t_lo", [P, NC, S], F32R)
        v_hi, v_lo = sb("v_hi", [P, NT, D], F32R), sb("v_lo", [P, NT, D], F32R)
        probs = sb("probs", [P, PROB_COLS])
        pT_hi, pT_lo = sb("pT_hi", [P, PROB_COLS], F32R), sb("pT_lo", [P, PROB_COLS], F32R)
        relu = sb("relu", [P, NC, S])
        act = sb("act", [P, NC, S])
        act_hi, act_lo = sb("act_hi", [P, NC, S], F32R), sb("act_lo", [P, NC, S], F32R)
        gate = sb("gate", [P, NT, D])
        attn = sb("attn", [P, NT, D])
        ffn = sb("ffn", [P, NT, D])
        y = sb("y", [P, NT, D])
        stats = sb("stats", [P, NT, 6])
        mv = sb("mv", [P, NT, 2])
        var_eps, rstd = sb("var_eps", [P, NT]), sb("rstd", [P, NT])
        neg_half = sb("neg_half", [P, NT])
        neg_max, row_sum, inv_sum = sb("neg_max", [P, NT]), sb("row_sum", [P, NT]), sb("inv_sum", [P, NT])
        ident = sb("ident", [P, P])
        mask = sb("mask", [P, 3 * P])
        ident_r, mask_r = sb("ident_r", [P, P], F32R), sb("mask_r", [P, 3 * P], F32R)
        raw = {n: sb(f"raw_{n}", [P, NC, D]) for n in ("q", "k", "v")}
        raw.update({"r": ffn[:, 0:2, :], "vf": ffn[:, 2:4, :], "kf": y[:, 0:2, :]})
        QKV = {"q": 0, "k": 1, "v": 2}
        bias, shift = sb("bias", [P, 3, NC]), sb("shift", [P, 3, NC])
        row_total, neg_mean_w = sb("row_total", [P, 3, NC]), sb("neg_mean_w", [P, 3, NC])
        mu = {n: sb(f"mu_{n}", [P, NC]) for n in ("r", "k")}
        scratch = {"q": gate[:, 0:2, :], "k": gate[:, 2:4, :], "v": attn[:, 0:2, :]}
        w_hi = {n: sb(f"w_hi_{n}", [P, NC, D], F32R) for n in ("m", "v", "kf", "r", "vf")}
        w_lo = {n: sb(f"w_lo_{n}", [P, NC, D], F32R) for n in ("m", "v", "kf", "r", "vf")}

        psum = ctx.enter_context(nc.psum_tensor("psum", [P, 8, 512], F32))

        def tile_of(banks, i):
            return psum[:, banks[i // 2], (i % 2) * D:(i % 2 + 1) * D]

        def score_tile(i, cols):
            bank, at = SCORES[i]
            return psum[:, bank, at:at + cols]

        def f32(ap):
            return ap.bitcast(F32)

        x_loaded = sem("x_loaded")
        x0_loaded = [sem(f"x0_loaded_{h}") for h in range(2)]
        y_stored = sem("y_stored")
        w_loaded = {n: sem(f"w_loaded_{n}") for n in ("q", "k", "v", "kf", "r", "vf")}
        b_loaded = {n: sem(f"b_loaded_{n}") for n in ("q", "k", "v")}
        mu_loaded = sem("mu_loaded")
        consts_ready, zeroed = sem("consts_ready"), sem("zeroed")
        stats_ready, mv_ready = sem("stats_ready"), sem("mv_ready")
        var_ready, rstd_ready = sem("var_ready"), sem("rstd_ready")
        xn_ready = sem("xn_ready")
        xT_ready = sem("xT_ready")
        xT_copied, x_hi_ready, x_lo_ready = sem("xT_copied"), sem("x_hi_ready"), sem("x_lo_ready")
        diff_ready = sem("diff_ready")
        mixk_ready, mixk_hi_ready, mixk_lo_ready = sem("mixk_ready"), sem("mixk_hi_ready"), sem("mixk_lo_ready")
        mixr_ready, mixr_hi_ready, mixr_lo_ready = sem("mixr_ready"), sem("mixr_hi_ready"), sem("mixr_lo_ready")
        t_ready, t_hi_ready, t_lo_ready = sem("t_ready"), sem("t_hi_ready"), sem("t_lo_ready")
        v_ready, v_hi_ready, v_lo_ready = sem("v_ready"), sem("v_hi_ready"), sem("v_lo_ready")
        scores_ready, max_ready, exp_ready = sem("scores_ready"), sem("max_ready"), sem("exp_ready")
        pT_ready, pT_hi_ready, pT_lo_ready = sem("pT_ready"), sem("pT_hi_ready"), sem("pT_lo_ready")
        inv_ready = sem("inv_ready")
        attn_ready, attn_added = sem("attn_ready"), sem("attn_added")
        key_ready, relu_ready = sem("key_ready"), sem("relu_ready")
        act_ready, act_hi_ready, act_lo_ready = sem("act_ready"), sem("act_hi_ready"), sem("act_lo_ready")
        gate_ready, tanh_ready = sem("gate_ready"), sem("tanh_ready")
        ffn_ready, ffn_gated = sem("ffn_ready"), sem("ffn_gated")
        y_ready = sem("y_ready")
        total_ready, mean_ready, shift_ready = sem("total_ready"), sem("mean_ready"), sem("shift_ready")
        w_shifted = {n: sem(f"w_shifted_{n}") for n in ("q", "k", "v")}
        w_ready, w_hi_ready, w_lo_ready = sem("w_ready"), sem("w_hi_ready"), sem("w_lo_ready")
        w_whole_ready, mix_w_lo_ready = sem("w_whole_ready"), sem("mix_w_lo_ready")

        W_BANK = {"kf": 0, "m": 5, "v": 6, "r": 1, "vf": 2}
        W_SCALE = {"m": 1.0, "v": 1.0, "kf": 1.0, "r": 1.0, "vf": 0.5}
        W_AT = {n: i + 1 for i, n in enumerate(W_BANK)}
        LO_AT = {"m": 1, "v": 2}
        MIX_AT = {"kf": 1, "r": 2, "vf": 3}

        block = ctx.enter_context(nc.Block())

        x_v = x.rearrange("b (t p) d -> b p t d", p=P)
        out_v = out.rearrange("b (t p) d -> b p t d", p=P)

        @block.sync
        def _(sp):
            for h in range(2):
                sp.dma_start(x_all[:, 0, 2 * h:2 * h + 2, :], x_v[0, :, 2 * h:2 * h + 2, :]).then_inc(x0_loaded[h], 16)
            def load_w(n, w_in):
                sp.dma_start(raw[n][:, :, :], w_in.rearrange("(o p) c -> p o c", p=P)).then_inc(w_loaded[n], 16)

            load_w("kf", Wkf)
            load_w("v", Wv)
            load_w("r", Wr)
            load_w("vf", Wvf)
            sp.dma_start(x_all[:, 1, :, :], x_v[1]).then_inc(x_loaded, 16)

            def turn(b, load, halves=1):
                if load:
                    sp.wait_ge(x_loaded, 16 * b + 16)
                    sp.dma_start(x_all[:, b + 2, :, :], x_v[b + 2]).then_inc(x_loaded, 16)
                k = NT // halves
                for h in range(halves):
                    sp.wait_ge(y_ready, 2 * b + 2 - (halves - 1 - h))
                    sp.dma_start(out_v[b, :, h * k:(h + 1) * k, :], y[:, h * k:(h + 1) * k, :]).then_inc(y_stored, 16)

            turn(0, load=True)
            with sp.Fori(*LOOP) as b:
                turn(b, load=True)
            turn(B - 2, load=False)
            turn(B - 1, load=False, halves=2)
            sp.wait_ge(y_stored, 16 * (B + 1))

        @block.tensor
        def _(pe):
            def three_passes(dst, parts, end=True):
                ops = []
                for (s_hi, s_lo), (m_hi, m_lo) in parts:
                    ops += [(s_hi, m_hi), (s_hi, m_lo), (s_lo, m_hi)]
                for n, (s, m) in enumerate(ops):
                    last = nc.tensor.matmul(dst, s, m, start=(n == 0), stop=end and n == len(ops) - 1,
                                            skip_group_check=not end)
                return last

            def halves(hi, lo, c, cols):
                return hi[:, c, cols], lo[:, c, cols]

            def transpose_x(b, first=False):
                pe.wait_ge(xn_ready, 4 * b + 4)
                if not first:
                    pe.wait_ge(tanh_ready, 2 * b - 2)
                for c in range(NC):
                    for i in range(NT):
                        last = nc.tensor.transpose(psum[:, XT_BANK[c], i * P:(i + 1) * P],
                                                   xn[:, i, c * P:(c + 1) * P], ident[:, :])
                    last.then_inc(xT_ready, 1)

            def project_t(b, first=False):
                pe.wait_ge(x_lo_ready, 2 * b + 2)
                pe.wait_ge(x_hi_ready, 2 * b + 2)
                for d in range(NC):
                    if not first:
                        pe.wait_ge(attn_added, 4 * b - 2 + 2 * d)
                    elif d == 1:
                        pe.wait_ge(xT_copied, NC)
                    three_passes(psum[:, T_BANK[d], :], [
                        (halves(w_hi["m"], w_lo["m"], c, slice(d * P, (d + 1) * P)), halves(x_hi, x_lo, c, slice(0, S)))
                        for c in range(NC)]).then_inc(t_ready, 1)

            def project_v(b, first=False):
                for i in range(NT):
                    if i % 2 == 0 and not first:
                        pe.wait_ge(ffn_gated, 2 * b - 1 + i // 2)
                    last = three_passes(tile_of(V_BANK, i), [
                        (halves(x_hi, x_lo, c, slice(i * P, (i + 1) * P)), halves(w_hi["v"], w_lo["v"], c, slice(0, D)))
                        for c in range(NC)])
                    if i % 2 == 1:
                        last.then_inc(v_ready, 1)

            def transpose_w(n):
                for c in range(NC):
                    for o in range(NC):
                        last = nc.tensor.transpose(psum[:, W_BANK[n], c * D + o * P:c * D + (o + 1) * P],
                                                   raw[n][:, o, c * P:(c + 1) * P], ident[:, :])
                last.then_inc(w_ready, 1)

            pe.wait_ge(zeroed, 1)
            for _ in range(WARM_UP):
                nc.tensor.matmul(psum[:, 7, 0:2 * P], probs[:, 0:P], probs[:, 0:2 * P], start=True, stop=True)
            pe.wait_ge(consts_ready, 4)
            pe.wait_ge(w_loaded["kf"], 16)
            transpose_w("kf")
            pe.wait_ge(w_shifted["q"], 2)
            pe.wait_ge(w_shifted["k"], 2)
            for c in range(NC):
                for o in range(NC):
                    last = nc.tensor.matmul(psum[:, W_BANK["m"], c * D:(c + 1) * D], raw["k"][:, o, c * P:(c + 1) * P],
                                            raw["q"][:, o, :], start=(o == 0), stop=(o == NC - 1))
            last.then_inc(w_ready, 1)
            transpose_x(0, first=True)
            pe.wait_ge(w_shifted["v"], 2)
            transpose_w("v")
            for n in ("r", "vf"):
                pe.wait_ge(w_loaded[n], 16)
                transpose_w(n)
            pe.wait_ge(w_lo_ready, LO_AT["m"])
            project_t(0, first=True)
            pe.wait_ge(w_lo_ready, LO_AT["v"])
            project_v(0, first=True)

            def turn(b, following, first=False):
                pe.wait_ge(t_lo_ready, 2 * b + 2)
                for i in SCORE_ORDER:
                    if first and i > 0:
                        pe.wait_ge(w_whole_ready, 4 - i)
                    if i == 1:
                        pe.wait_ge(tanh_ready, 2 * b)
                    if i > 0:
                        three_passes(score_tile(i, (i + 1) * P), [
                            (halves(x_hi, x_lo, c, slice(i * P, (i + 1) * P)), halves(t_hi, t_lo, c, slice(0, (i + 1) * P)))
                            for c in range(NC)], end=False)
                    else:
                        for c in range(NC):
                            nc.tensor.matmul(score_tile(0, P), x_first[:, c, :], t_first[:, c, :], start=False, stop=False,
                                             skip_group_check=True)
                    if i != 1:
                        bank, at = SCORES[max(i, 1)]
                        at += (max(i, 1) - (i > 1)) * P
                        which = slice(0, 2 * P) if i > 1 else slice(P, 3 * P)
                        if first and i == 3:
                            pe.wait_ge(consts_ready, 6)
                        nc.tensor.matmul(psum[:, bank, at:at + 2 * P], ident_r[:, :], mask_r[:, which], start=False,
                                         stop=True, skip_group_check=True).then_inc(scores_ready, 1)
                if following:
                    transpose_x(b + 1)
                if first:
                    pe.wait_ge(mix_w_lo_ready, MIX_AT["kf"])
                pe.wait_ge(mixk_lo_ready, b + 1)
                pe.wait_ge(v_lo_ready, 2 * b + 1)
                for o in range(NC):
                    three_passes(psum[:, KEY_BANK[o], :], [
                        (halves(w_hi["kf"], w_lo["kf"], c, slice(o * P, (o + 1) * P)), halves(mixk_hi, mixk_lo, c, slice(0, S)))
                        for c in range(NC)]).then_inc(key_ready, 1)
                pe.wait_ge(v_lo_ready, 2 * b + 2)
                for g, tiles in enumerate(PROB_TILES):
                    if g == 0:
                        pe.wait_ge(exp_ready, 4 * b + 1)
                    if g == 1:
                        pe.wait_ge(exp_ready, 4 * b + 4)
                    for i in tiles:
                        for j in range(i + 1):
                            at = PROB_AT[i] + j * P
                            last = nc.tensor.transpose(psum[:, PROB_BANK[g], at % 512:at % 512 + P],
                                                       probs[:, at:at + P], ident[:, :])
                    last.then_inc(pT_ready, 1)
                if first:
                    pe.wait_ge(mix_w_lo_ready, MIX_AT["r"])
                pe.wait_ge(mixr_lo_ready, b + 1)
                if following:
                    pe.wait_ge(x_hi_ready, 2 * b + 4)
                for i in range(NT):
                    last = three_passes(tile_of(GATE_BANK, i), [
                        (halves(mixr_hi, mixr_lo, c, slice(i * P, (i + 1) * P)), halves(w_hi["r"], w_lo["r"], c, slice(0, D)))
                        for c in range(NC)])
                    if i % 2 == 1:
                        last.then_inc(gate_ready, 1)
                pe.wait_ge(relu_ready, 2 * b + 2)
                for n, i in enumerate((3, 2, 0, 1)):
                    if i > 0:
                        pe.wait_ge(pT_lo_ready, 3 * b + (3, 2, 1)[i - 1])
                    last = three_passes(tile_of(ATTN_BANK, i), [
                        ((pT_hi[:, PROB_AT[i] + j * P:PROB_AT[i] + (j + 1) * P], pT_lo[:, PROB_AT[i] + j * P:PROB_AT[i] + (j + 1) * P]),
                         (v_hi[:, j, :], v_lo[:, j, :])) for j in range(i + 1)])
                    if n % 2 == 1:
                        last.then_inc(attn_ready, 1)
                if first:
                    pe.wait_ge(mix_w_lo_ready, MIX_AT["vf"])
                pe.wait_ge(act_lo_ready, 2 * b + 2)
                for i in range(NT):
                    last = three_passes(tile_of(FFN_BANK, i), [
                        (halves(act_hi, act_lo, c, slice(i * P, (i + 1) * P)), halves(w_hi["vf"], w_lo["vf"], c, slice(0, D)))
                        for c in range(NC)])
                    if i % 2 == 1:
                        last.then_inc(ffn_ready, 1)
                if following:
                    project_t(b + 1)
                    project_v(b + 1)

            turn(0, True, first=True)
            with pe.Fori(*LOOP) as b:
                turn(b, True)
            turn(B - 2, True)
            turn(B - 1, False)

        @block.scalar
        def _(sc):
            for n, w_in in (("q", Wq), ("k", Wk)):
                sc.dma_start(raw[n][:, :, :], w_in.rearrange("(o p) c -> p o c", p=P)).then_inc(w_loaded[n], 16)
            sc.preload_act_table(ACT.Exp)
            for n in ("q", "k", "v"):
                sc.wait_ge(w_loaded[n], 16)
                for o in range(NC):
                    nc.scalar.activation(scratch[n][:, o, :], raw[n][:, o, :], ACT.Copy,
                                         accum_out=row_total[:, QKV[n], o:o + 1]).then_inc(total_ready, 1)

            def whole_x(c):
                nc.scalar.activation(x_first[:, c, :], psum[:, XT_BANK[c], 0:P], ACT.Copy, bias=UNIT)
                nc.scalar.activation(xT[:, c, 1:S + 1], psum[:, XT_BANK[c], :], ACT.Copy).then_inc(xT_copied, 1)

            def upper_x(c):
                nc.scalar.activation(x_hi[:, c, :], psum[:, XT_BANK[c], :], ACT.Copy, bias=UNIT).then_inc(x_hi_ready, 1)

            def copy_x(b):
                sc.wait_ge(mixr_ready, b)
                for c in range(NC):
                    sc.wait_ge(xT_ready, 2 * b + c + 1)
                    whole_x(c)
                    upper_x(c)

            def upper_mix(b, src, dst, src_ready, dst_ready, read):
                sc.wait_ge(src_ready, b + 1)
                sc.wait_ge(read, 2 * b)
                nc.scalar.activation(dst[:, :, :], src[:, :, :], ACT.Copy).then_inc(dst_ready, 1)

            def upper_t(b):
                for d in range(NC):
                    sc.wait_ge(t_ready, 2 * b + d + 1)
                    nc.scalar.activation(t_first[:, d, :], psum[:, T_BANK[d], 0:P], ACT.Copy)
                    nc.scalar.activation(t_hi[:, d, :], psum[:, T_BANK[d], :], ACT.Copy).then_inc(t_hi_ready, 1)

            def upper_v(b):
                for h in range(2):
                    sc.wait_ge(v_ready, 2 * b + h + 1)
                    nc.scalar.activation(v_hi[:, 2 * h:2 * h + 2, :], psum[:, V_BANK[h], :].rearrange("p (t d) -> p t d", d=D),
                                         ACT.Copy).then_inc(v_hi_ready, 1)

            def upper_w(n):
                sc.wait_ge(w_ready, W_AT[n])
                nc.scalar.activation(w_hi[n][:, :, :], psum[:, W_BANK[n], :].rearrange("p (c o) -> p c o", o=D),
                                     ACT.Copy, scale=W_SCALE[n]).then_inc(w_hi_ready, 1)

            def whole_w(n):
                nc.scalar.activation(raw[n][:, :, :], psum[:, W_BANK[n], :].rearrange("p (c o) -> p c o", o=D),
                                     ACT.Copy, scale=W_SCALE[n]).then_inc(w_whole_ready, 1)

            upper_w("kf")
            whole_w("kf")
            upper_w("m")
            for c in range(NC):
                sc.wait_ge(xT_ready, c + 1)
                upper_x(c)
            for c in range(NC):
                sc.wait_ge(x_lo_ready, c + 1)
                whole_x(c)
            upper_w("v")
            upper_t(0)
            upper_w("r")
            whole_w("r")
            upper_w("vf")
            whole_w("vf")
            upper_v(0)
            upper_mix(0, mixk, mixk_hi, mixk_ready, mixk_hi_ready, key_ready)

            def turn(b, following, first=False):
                for n, i in enumerate(SCORE_ORDER):
                    sc.wait_ge(max_ready, 3 * b + min(n, 2) + 1)
                    nc.scalar.activation(probs[:, PROB_AT[i]:PROB_AT[i] + (i + 1) * P], score_tile(i, (i + 1) * P), ACT.Exp,
                                         bias=neg_max[:, i:i + 1], accum_out=row_sum[:, i:i + 1]).then_inc(exp_ready, 1)
                if first:
                    upper_mix(0, mixr, mixr_hi, mixr_ready, mixr_hi_ready, gate_ready)
                if following:
                    copy_x(b + 1)
                sc.wait_ge(act_ready, 2 * b)
                for o in range(NC):
                    sc.wait_ge(key_ready, 2 * b + o + 1)
                    nc.scalar.activation(relu[:, o, :], psum[:, KEY_BANK[o], :], ACT.Relu).then_inc(relu_ready, 1)
                for g, (lo, hi) in enumerate(PROB_GROUPS):
                    sc.wait_ge(pT_ready, 3 * b + g + 1)
                    nc.scalar.activation(pT_hi[:, lo:hi], psum[:, PROB_BANK[g], 0:hi - lo], ACT.Copy).then_inc(pT_hi_ready, 1)
                for o in range(NC):
                    sc.wait_ge(act_ready, 2 * b + o + 1)
                    nc.scalar.activation(act_hi[:, o, :], act[:, o, :], ACT.Copy).then_inc(act_hi_ready, 1)
                sc.wait_ge(ffn_gated, 2 * b)
                for h in range(2):
                    sc.wait_ge(gate_ready, 2 * b + h + 1)
                    nc.scalar.activation(gate[:, 2 * h:2 * h + 2, :], psum[:, GATE_BANK[h], :].rearrange("p (t d) -> p t d", d=D),
                                         ACT.Tanh, scale=0.5).then_inc(tanh_ready, 1)
                if following:
                    upper_mix(b + 1, mixk, mixk_hi, mixk_ready, mixk_hi_ready, key_ready)
                    upper_mix(b + 1, mixr, mixr_hi, mixr_ready, mixr_hi_ready, gate_ready)
                    upper_t(b + 1)
                    upper_v(b + 1)

            turn(0, True, first=True)
            with sc.Fori(*LOOP) as b:
                turn(b, True)
            turn(B - 2, True)
            turn(B - 1, False)

        @block.vector
        def _(dv):
            def statistics(b, loaded):
                for t in range(NT):
                    loaded(t)
                    nc.vector.bn_stats(stats[:, t, :], x_all[:, b, t, :]).then_inc(stats_ready, 1)

            def aggregate(b):
                for t in range(NT):
                    nc.vector.bn_aggr(mv[:, t, :], stats[:, t, :]).then_inc(mv_ready, 1)
                dv.wait_ge(mv_ready, 4 * b + 4)
                nc.vector.tensor_scalar(var_eps[:, :], mv[:, :, 1], EPS, None, ALU.add).then_inc(var_ready, 1)

            def normalise(b):
                dv.wait_ge(rstd_ready, b + 1)
                dv.wait_ge(xT_ready, 2 * b)
                for t in range(NT):
                    nc.vector.tensor_scalar(xn[:, t, :], x_all[:, b, t, :], mv[:, t, 0:1], rstd[:, t:t + 1],
                                            ALU.subtract, ALU.mult).then_inc(xn_ready, 1)

            def difference(b):
                dv.wait_ge(xT_copied, 2 * b + 2)
                nc.vector.tensor_tensor(diff[:, :, :], xT[:, :, 1:S + 1], xT[:, :, 0:S], ALU.subtract).then_inc(diff_ready, 1)

            def lower_x(b, whole):
                for c in range(NC):
                    dv.wait_ge(x_hi_ready, 2 * b + c + 1)
                    nc.vector.scalar_tensor_tensor(out=x_lo[:, c, :], in0=whole(c), scalar=UNIT, in1=f32(x_hi[:, c, :]),
                                                   op0=ALU.add, op1=ALU.subtract).then_inc(x_lo_ready, 1)

            def mix(b, m, dst, ready, lo_ready):
                dv.wait_ge(diff_ready, b + 1)
                dv.wait_ge(lo_ready, b)
                for c in range(NC):
                    last = nc.vector.scalar_tensor_tensor(out=dst[:, c, :], in0=diff[:, c, :], scalar=mu[m][:, c:c + 1],
                                                          in1=xT[:, c, 0:S], op0=ALU.mult, op1=ALU.add)
                last.then_inc(ready, 1)

            def lower_t(b, chunks=range(NC)):
                for d in chunks:
                    dv.wait_ge(t_hi_ready, 2 * b + d + 1)
                    nc.vector.tensor_tensor(t_lo[:, d, :], psum[:, T_BANK[d], :], f32(t_hi[:, d, :]),
                                            ALU.subtract).then_inc(t_lo_ready, 1)

            def lower_v(b):
                for h in range(2):
                    dv.wait_ge(v_hi_ready, 2 * b + h + 1)
                    nc.vector.tensor_tensor(v_lo[:, 2 * h:2 * h + 2, :], psum[:, V_BANK[h], :].rearrange("p (t d) -> p t d", d=D),
                                            f32(v_hi[:, 2 * h:2 * h + 2, :]), ALU.subtract).then_inc(v_lo_ready, 1)

            def lower_w(n):
                dv.wait_ge(w_hi_ready, W_AT[n])
                nc.vector.scalar_tensor_tensor(out=w_lo[n][:, :, :], in0=psum[:, W_BANK[n], :].rearrange("p (c o) -> p c o", o=D),
                                               scalar=W_SCALE[n], in1=f32(w_hi[n][:, :, :]), op0=ALU.mult,
                                               op1=ALU.subtract).then_inc(w_lo_ready, 1)

            def prepare(names, at):
                these = slice(QKV[names[0]], QKV[names[-1]] + 1)
                dv.wait_ge(total_ready, NC * (QKV[names[-1]] + 1))
                nc.vector.tensor_scalar(neg_mean_w[:, these, :], row_total[:, these, :], -1.0 / D, None, ALU.mult).then_inc(mean_ready, 1)
                for n in names:
                    dv.wait_ge(b_loaded[n], 16)
                dv.wait_ge(mean_ready, at)
                nc.vector.scalar_tensor_tensor(out=shift[:, these, :], in0=bias[:, these, :], scalar=UNIT,
                                               in1=neg_mean_w[:, these, :], op0=ALU.mult, op1=ALU.add).then_inc(shift_ready, 1)
                dv.wait_ge(shift_ready, at)
                for n in names:
                    for o in range(NC):
                        nc.vector.tensor_scalar(raw[n][:, o, :], raw[n][:, o, :], shift[:, QKV[n], o:o + 1],
                                                UNIT if n == "q" else 1.0, ALU.add, ALU.mult).then_inc(w_shifted[n], 1)

            statistics(0, lambda t: dv.wait_ge(x0_loaded[t // 2], 16))
            dv.wait_ge(stats_ready, 4)
            aggregate(0)
            prepare(("q", "k"), 1)
            normalise(0)
            dv.wait_ge(consts_ready, 4)
            nc.vector.tensor_copy(ident_r[:, :], ident[:, :]).then_inc(consts_ready, 1)
            nc.vector.tensor_copy(mask_r[:, :], mask[:, :]).then_inc(consts_ready, 1)
            prepare(("v",), 2)
            lower_w("m")
            lower_x(0, lambda c: psum[:, XT_BANK[c], :])
            statistics(1, lambda t: dv.wait_ge(x_loaded, 16))
            lower_w("v")
            dv.wait_ge(stats_ready, 8)
            aggregate(1)
            lower_t(0, (0,))
            dv.wait_ge(mu_loaded, 32)
            mix(0, "k", mixk, mixk_ready, mixk_lo_ready)
            lower_t(0, (1,))
            normalise(1)
            lower_v(0)

            def turn(b, following, after_next, first=False):
                for n, i in enumerate(SCORE_ORDER):
                    if i > 0:
                        dv.wait_ge(scores_ready, 3 * b + n + 1)
                    last = nc.vector.tensor_reduce(neg_max[:, i:i + 1], score_tile(i, (i + 1) * P), AX.X, ALU.max,
                                                   negate=True)
                    if i != 1:
                        last.then_inc(max_ready, 1)
                if first:
                    mix(0, "r", mixr, mixr_ready, mixr_lo_ready)
                if after_next:
                    statistics(b + 2, lambda t: dv.wait_ge(x_loaded, 16 * b + 32) if t == 0 else None)
                if following:
                    difference(b + 1)
                for g, (lo, hi) in enumerate(PROB_GROUPS):
                    dv.wait_ge(pT_hi_ready, 3 * b + g + 1)
                    nc.vector.tensor_tensor(pT_lo[:, lo:hi], psum[:, PROB_BANK[g], 0:hi - lo], f32(pT_hi[:, lo:hi]),
                                            ALU.subtract).then_inc(pT_lo_ready, 1)
                if after_next:
                    dv.wait_ge(stats_ready, 4 * b + 12)
                if following:
                    lower_x(b + 1, lambda c: xT[:, c, 1:S + 1])
                if after_next:
                    aggregate(b + 2)
                if following:
                    mix(b + 1, "k", mixk, mixk_ready, mixk_lo_ready)
                    mix(b + 1, "r", mixr, mixr_ready, mixr_lo_ready)
                dv.wait_ge(exp_ready, 4 * b + 4)
                nc.vector.reciprocal(inv_sum[:, :], row_sum[:, :]).then_inc(inv_ready, 1)
                dv.wait_ge(inv_ready, b + 1)
                for n, i in enumerate((3, 2, 0, 1)):
                    dv.wait_ge(attn_ready, 2 * b + n // 2 + 1)
                    nc.vector.scalar_tensor_tensor(out=attn[:, i, :], in0=tile_of(ATTN_BANK, i), scalar=inv_sum[:, i:i + 1],
                                                   in1=x_all[:, b, i, :], op0=ALU.mult, op1=ALU.add).then_inc(attn_added, 1)
                dv.wait_ge(tanh_ready, 2 * b + 2)
                dv.wait_ge(attn_added, 4 * b + 4)
                dv.wait_ge(y_stored, 16 * b)
                for h in range(2):
                    two = slice(2 * h, 2 * h + 2)
                    dv.wait_ge(ffn_ready, 2 * b + h + 1)
                    nc.vector.scalar_tensor_tensor(out=ffn[:, two, :], in0=gate[:, two, :], scalar=1.0,
                                                   in1=psum[:, FFN_BANK[h], :].rearrange("p (t d) -> p t d", d=D),
                                                   op0=ALU.add, op1=ALU.mult).then_inc(ffn_gated, 1)
                    dv.wait_ge(ffn_gated, 2 * b + h + 1)
                    nc.vector.tensor_tensor(y[:, two, :], attn[:, two, :], ffn[:, two, :], ALU.add).then_inc(y_ready, 1)
                if following:
                    lower_t(b + 1)
                if after_next:
                    normalise(b + 2)
                if following:
                    lower_v(b + 1)

            turn(0, True, True, first=True)
            with dv.Fori(*LOOP) as b:
                turn(b, True, True)
            turn(B - 2, True, False)
            turn(B - 1, False, False)

        @block.gpsimd
        def _(gp):
            def load_bias(n, b_in):
                gp.dma_start(bias[:, QKV[n], :], b_in.rearrange("(o p) -> p o", p=P),
                             allow_slow_non_contiguous=True).then_inc(b_loaded[n], 16)

            gp.memset(probs[:, 0:2 * P], 0.0).then_inc(zeroed, 1)
            gp.memset(neg_half[:, :], -0.5).then_inc(consts_ready, 1)
            gp.memset(xT[:, :, 0:1], 0.0).then_inc(consts_ready, 1)
            load_bias("q", bq)
            load_bias("k", bk)
            load_bias("v", bv)
            for tile in (ident, mask):
                gp.memset(tile[:, :], 0.0).then_inc(zeroed, 1)
            gp.wait_ge(zeroed, 3)
            gp.affine_select(out=ident[:, :], in_=ident[:, :], compare_op=ALU.not_equal, fill=1.0, base=0,
                             pattern=[[-1, P]], channel_multiplier=1).then_inc(consts_ready, 1)
            causal = mask[:, P:3 * P].rearrange("p (a k) -> p a k", k=P)
            gp.affine_select(out=causal, in_=causal, compare_op=ALU.is_ge, fill=MASKED, base=0,
                             pattern=[[0, 2], [-1, P]], channel_multiplier=1).then_inc(consts_ready, 1)

            def inverse_deviation(b):
                gp.wait_ge(var_ready, b + 1)
                nc.gpsimd.tensor_tensor(rstd[:, :], var_eps[:, :], neg_half[:, :], ALU.pow).then_inc(rstd_ready, 1)

            def lower(b, whole, hi, lo, hi_ready, lo_ready):
                gp.wait_ge(hi_ready, b + 1)
                nc.gpsimd.tensor_tensor(lo[:, :, :], whole[:, :, :], f32(hi[:, :, :]), ALU.subtract).then_inc(lo_ready, 1)

            inverse_deviation(0)
            for n, m_in in (("k", mu_k), ("r", mu_r)):
                gp.dma_start(mu[n][:, :], m_in.rearrange("(c p) -> p c", p=P), allow_slow_non_contiguous=True).then_inc(mu_loaded, 16)
            def lower_w(n):
                gp.wait_ge(w_whole_ready, MIX_AT[n])
                nc.gpsimd.tensor_tensor(w_lo[n][:, :, :], raw[n][:, :, :], f32(w_hi[n][:, :, :]),
                                        ALU.subtract).then_inc(mix_w_lo_ready, 1)

            lower_w("kf")
            gp.wait_ge(xT_copied, 2)
            nc.gpsimd.tensor_tensor(diff[:, :, :], xT[:, :, 1:S + 1], xT[:, :, 0:S], ALU.subtract).then_inc(diff_ready, 1)
            inverse_deviation(1)
            lower_w("r")
            lower(0, mixk, mixk_hi, mixk_lo, mixk_hi_ready, mixk_lo_ready)
            lower_w("vf")
            lower(0, mixr, mixr_hi, mixr_lo, mixr_hi_ready, mixr_lo_ready)

            def turn(b, following, after_next):
                for o in range(NC):
                    gp.wait_ge(relu_ready, 2 * b + o + 1)
                    if o == 0:
                        gp.wait_ge(act_hi_ready, 2 * b)
                        gp.wait_ge(act_lo_ready, 2 * b)
                    nc.gpsimd.tensor_tensor(act[:, o, :], relu[:, o, :], relu[:, o, :], ALU.mult).then_inc(act_ready, 1)
                for o in range(NC):
                    gp.wait_ge(act_hi_ready, 2 * b + o + 1)
                    nc.gpsimd.tensor_tensor(act_lo[:, o, :], act[:, o, :], f32(act_hi[:, o, :]),
                                            ALU.subtract).then_inc(act_lo_ready, 1)
                if following:
                    lower(b + 1, mixk, mixk_hi, mixk_lo, mixk_hi_ready, mixk_lo_ready)
                if after_next:
                    inverse_deviation(b + 2)
                if following:
                    lower(b + 1, mixr, mixr_hi, mixr_lo, mixr_hi_ready, mixr_lo_ready)

            turn(0, True, True)
            with gp.Fori(*LOOP) as b:
                turn(b, True, True)
            turn(B - 2, True, False)
            turn(B - 1, False, False)


_INS = ["L0_attn_x", "L0_attn_Wk", "L0_attn_bk", "L0_attn_Wq", "L0_attn_bq", "L0_attn_Wv", "L0_attn_bv",
        "L0_ffn_W_r", "L0_ffn_W_k", "L0_ffn_W_v", "L0_ffn_mu_r", "L0_ffn_mu_k"]


def kernel(**inputs):
    import numpy as _np
    import concourse.bacc as _bacc
    from concourse import mybir as _mybir
    from concourse.bass_utils import run_bass_kernel_spmd as _run

    nc = _bacc.Bacc("TRN2", target_bir_lowering=False, num_devices=1)
    arrays, args = {}, []
    for name in _INS:
        a = _np.ascontiguousarray(inputs[name])
        arrays[f"in_{name}"] = a
        args.append(nc.dram_tensor(f"in_{name}", a.shape, _mybir.dt.from_np(a.dtype), kind="ExternalInput").ap())
    out = nc.dram_tensor("out_0", inputs["L0_attn_x"].shape, _mybir.dt.float32, kind="ExternalOutput").ap()
    attention_and_channel_mix_kernel(nc, *args, out)
    r = _run(nc, [arrays], core_ids=[0])
    return r.results[0]["out_0"]
```

```python
from concourse import mybir
from contextlib import ExitStack


def attention_and_channel_mix_kernel(nc, x, Wk, bk, Wq, bq, Wv, bv, Wr, Wkf, Wvf, mu_r, mu_k, out):
    F32 = mybir.dt.float32
    F32R = mybir.dt.float32r
    ALU = mybir.AluOpType
    ACT = mybir.ActivationFunctionType
    AX = mybir.AxisListType

    B, S, D = x.shape
    P = 128
    NT = S // P
    NC = D // P
    EPS = 1e-5
    UNIT = float(D) ** -0.5
    MASKED = -1e30
    WARM_UP = 6
    LOOP = (1, B - 2)

    PROB_AT = {3: 0, 2: 512, 0: 896, 1: 1024}
    PROB_COLS = 1280
    PROB_GROUPS = ((0, 512), (512, 1024), (1024, 1280))
    PROB_TILES = ((3,), (2, 0), (1,))
    SCORES = {3: (0, 0), 2: (1, 0), 1: (2, 0), 0: (2, 256)}
    SCORE_ORDER = (3, 2, 1, 0)
    XT_BANK = (3, 4)
    T_BANK = (5, 4)
    KEY_BANK = (5, 6)
    PROB_BANK = (7, 0, 1)
    GATE_BANK = (2, 3)
    ATTN_BANK = (4, 5)
    FFN_BANK = (6, 7)
    LAST_FFN_BANK = (6, 7, 0, 1)
    V_BANK = (6, 7)

    ctx = ExitStack()
    with ctx:
        def sb(name, shape, dt=F32):
            return ctx.enter_context(nc.sbuf_tensor(name, shape, dt))

        def sem(name):
            return ctx.enter_context(nc.semaphore(name))

        x_all = sb("x_all", [P, B, NT, D])
        xn = sb("xn", [P, NT, D])
        xT = sb("xT", [P, NC, S + 2])
        x_hi, x_lo = sb("x_hi", [P, NC, S], F32R), sb("x_lo", [P, NC, S], F32R)
        x_first, t_first = sb("x_first", [P, NC, P]), sb("t_first", [P, NC, P])
        diff = sb("diff", [P, NC, S])
        mixk, mixr = sb("mixk", [P, NC, S]), sb("mixr", [P, NC, S])
        mixk_hi, mixk_lo = sb("mixk_hi", [P, NC, S], F32R), sb("mixk_lo", [P, NC, S], F32R)
        mixr_hi, mixr_lo = sb("mixr_hi", [P, NC, S], F32R), sb("mixr_lo", [P, NC, S], F32R)
        t_hi, t_lo = sb("t_hi", [P, NC, S], F32R), sb("t_lo", [P, NC, S], F32R)
        v_hi, v_lo = sb("v_hi", [P, NT, D], F32R), sb("v_lo", [P, NT, D], F32R)
        probs = sb("probs", [P, PROB_COLS])
        pT_hi, pT_lo = sb("pT_hi", [P, PROB_COLS], F32R), sb("pT_lo", [P, PROB_COLS], F32R)
        relu = sb("relu", [P, NC, S])
        act = sb("act", [P, NC, S])
        act_hi, act_lo = sb("act_hi", [P, NC, S], F32R), sb("act_lo", [P, NC, S], F32R)
        gate = sb("gate", [P, NT, D])
        attn = sb("attn", [P, NT, D])
        ffn = sb("ffn", [P, NT, D])
        y = sb("y", [P, NT, D])
        stats = sb("stats", [P, NT, 6])
        mv = sb("mv", [P, NT, 2])
        var_eps, rstd = sb("var_eps", [P, NT]), sb("rstd", [P, NT])
        neg_half = sb("neg_half", [P, NT])
        neg_max, row_sum, inv_sum = sb("neg_max", [P, NT]), sb("row_sum", [P, NT]), sb("inv_sum", [P, NT])
        ident = sb("ident", [P, P])
        mask = sb("mask", [P, 2 * P])
        raw = {n: sb(f"raw_{n}", [P, NC, D]) for n in ("q", "k", "v")}
        raw.update({"r": ffn[:, 0:2, :], "vf": ffn[:, 2:4, :], "kf": y[:, 0:2, :]})
        QKV = {"q": 0, "k": 1, "v": 2}
        bias, shift = sb("bias", [P, 3, NC]), sb("shift", [P, 3, NC])
        row_total, neg_mean_w = sb("row_total", [P, 3, NC]), sb("neg_mean_w", [P, 3, NC])
        mu = {n: sb(f"mu_{n}", [P, NC]) for n in ("r", "k")}
        scratch = {"q": gate[:, 0:2, :], "k": gate[:, 2:4, :], "v": attn[:, 0:2, :]}
        w_hi = {n: sb(f"w_hi_{n}", [P, NC, D], F32R) for n in ("m", "v", "kf", "r", "vf")}
        w_lo = {n: sb(f"w_lo_{n}", [P, NC, D], F32R) for n in ("m", "v", "kf", "r", "vf")}

        psum = ctx.enter_context(nc.psum_tensor("psum", [P, 8, 512], F32))

        def tile_of(banks, i):
            return psum[:, banks[i // 2], (i % 2) * D:(i % 2 + 1) * D]

        def score_tile(i, cols):
            bank, at = SCORES[i]
            return psum[:, bank, at:at + cols]

        def f32(ap):
            return ap.bitcast(F32)

        x_loaded = sem("x_loaded")
        x0_loaded = [sem(f"x0_loaded_{h}") for h in range(2)]
        y_stored = sem("y_stored")
        w_loaded = {n: sem(f"w_loaded_{n}") for n in ("q", "k", "v", "kf", "r", "vf")}
        b_loaded = {n: sem(f"b_loaded_{n}") for n in ("q", "k", "v")}
        mu_loaded = sem("mu_loaded")
        zeroed, consts_ready = sem("zeroed"), sem("consts_ready")
        stats_ready, mv_ready = sem("stats_ready"), sem("mv_ready")
        var_ready, rstd_ready = sem("var_ready"), sem("rstd_ready")
        xn_ready = sem("xn_ready")
        xT_ready = sem("xT_ready")
        xT_copied, x_hi_ready, x_lo_ready = sem("xT_copied"), sem("x_hi_ready"), sem("x_lo_ready")
        diff_ready = sem("diff_ready")
        mixk_ready, mixk_hi_ready, mixk_lo_ready = sem("mixk_ready"), sem("mixk_hi_ready"), sem("mixk_lo_ready")
        mixr_ready, mixr_hi_ready, mixr_lo_ready = sem("mixr_ready"), sem("mixr_hi_ready"), sem("mixr_lo_ready")
        t_ready, t_hi_ready, t_lo_ready = sem("t_ready"), sem("t_hi_ready"), sem("t_lo_ready")
        v_ready, v_hi_ready, v_lo_ready = sem("v_ready"), sem("v_hi_ready"), sem("v_lo_ready")
        masked = sem("masked")
        scores_ready, max_ready, exp_ready = sem("scores_ready"), sem("max_ready"), sem("exp_ready")
        pT_ready, pT_hi_ready, pT_lo_ready = sem("pT_ready"), sem("pT_hi_ready"), sem("pT_lo_ready")
        inv_ready = sem("inv_ready")
        attn_ready, attn_added = sem("attn_ready"), sem("attn_added")
        key_ready, relu_ready = sem("key_ready"), sem("relu_ready")
        act_ready, act_hi_ready, act_lo_ready = sem("act_ready"), sem("act_hi_ready"), sem("act_lo_ready")
        gate_ready, tanh_ready = sem("gate_ready"), sem("tanh_ready")
        ffn_ready, ffn_gated = sem("ffn_ready"), sem("ffn_gated")
        y_ready = sem("y_ready")
        total_ready, mean_ready, shift_ready = sem("total_ready"), sem("mean_ready"), sem("shift_ready")
        w_shifted = {n: sem(f"w_shifted_{n}") for n in ("q", "k", "v")}
        w_ready, w_hi_ready, w_lo_ready = sem("w_ready"), sem("w_hi_ready"), sem("w_lo_ready")
        w_whole_ready, mix_w_lo_ready = sem("w_whole_ready"), sem("mix_w_lo_ready")

        W_BANK = {"kf": 0, "m": 5, "v": 6, "r": 1, "vf": 2}
        W_AT = {n: i + 1 for i, n in enumerate(W_BANK)}
        ATTN_W_AT = {"m": 1, "v": 2}
        MIX_W_AT = {"kf": 1, "r": 2, "vf": 3}
        W_SCALE = {"m": 1.0, "v": 1.0, "kf": 1.0, "r": 1.0, "vf": 0.5}

        def by_chunk(n):
            return psum[:, W_BANK[n], :].rearrange("p (c o) -> p c o", o=D)

        block = ctx.enter_context(nc.Block())

        x_v = x.rearrange("b (t p) d -> b p t d", p=P)
        out_v = out.rearrange("b (t p) d -> b p t d", p=P)

        @block.sync
        def _(sp):
            for h in range(2):
                sp.dma_start(x_all[:, 0, 2 * h:2 * h + 2, :], x_v[0, :, 2 * h:2 * h + 2, :]).then_inc(x0_loaded[h], 16)

            def load_w(n, w_in):
                sp.dma_start(raw[n][:, :, :], w_in.rearrange("(o p) c -> p o c", p=P)).then_inc(w_loaded[n], 16)

            load_w("kf", Wkf)
            load_w("v", Wv)
            load_w("r", Wr)
            load_w("vf", Wvf)

            def load(b):
                sp.dma_start(x_all[:, b, :, :], x_v[b]).then_inc(x_loaded, 16)

            def load_ahead(b):
                sp.wait_ge(x_loaded, 16 * b + 32)
                load(b + 3)

            def store(b):
                sp.wait_ge(y_ready, 2 * b + 2)
                sp.dma_start(out_v[b], y[:, :, :]).then_inc(y_stored, 16)

            load(1)
            sp.wait_ge(x_loaded, 16)
            load(2)
            load_ahead(0)
            store(0)
            with sp.Fori(LOOP[0], B - 3) as b:
                load_ahead(b)
                store(b)
            for b in (B - 3, B - 2):
                store(b)
            for t in range(NT):
                sp.wait_ge(y_ready, 2 * (B - 1) + t + 1)
                sp.dma_start(out_v[B - 1, :, t, :], y[:, t, :]).then_inc(y_stored, 16)
            sp.wait_ge(y_stored, 16 * (B - 1 + NT))

        @block.tensor
        def _(pe):
            def three_passes(dst, parts):
                for n, ((s_hi, s_lo), (m_hi, m_lo)) in enumerate(parts):
                    nc.tensor.matmul(dst, s_hi, m_hi, start=(n == 0), stop=False)
                    nc.tensor.matmul(dst, s_hi, m_lo, start=False, stop=False)
                    last = nc.tensor.matmul(dst, s_lo, m_hi, start=False, stop=(n == len(parts) - 1))
                return last

            def halves(hi, lo, c, cols):
                return hi[:, c, cols], lo[:, c, cols]

            def transpose_x(b, first=False):
                pe.wait_ge(xn_ready, 4 * b + 4)
                if not first:
                    pe.wait_ge(tanh_ready, 2 * b - 2)
                for c in range(NC):
                    for i in range(NT):
                        last = nc.tensor.transpose(psum[:, XT_BANK[c], i * P:(i + 1) * P],
                                                   xn[:, i, c * P:(c + 1) * P], ident[:, :])
                    last.then_inc(xT_ready, 1)

            def project_t(b, first=False):
                pe.wait_ge(x_hi_ready, 2 * b + 2)
                pe.wait_ge(x_lo_ready, 2 * b + 2)
                for d in range(NC):
                    if not first:
                        pe.wait_ge(attn_added, 4 * b - 2 + 2 * d)
                    elif d == 1:
                        pe.wait_ge(xT_copied, NC)
                    three_passes(psum[:, T_BANK[d], :], [
                        (halves(w_hi["m"], w_lo["m"], c, slice(d * P, (d + 1) * P)), halves(x_hi, x_lo, c, slice(0, S)))
                        for c in range(NC)]).then_inc(t_ready, 1)

            def project_v(b, first=False):
                for i in range(NT):
                    if i % 2 == 0 and not first:
                        pe.wait_ge(ffn_gated, 2 * b - 1 + i // 2)
                    last = three_passes(tile_of(V_BANK, i), [
                        (halves(x_hi, x_lo, c, slice(i * P, (i + 1) * P)), halves(w_hi["v"], w_lo["v"], c, slice(0, D)))
                        for c in range(NC)])
                    if i % 2 == 1:
                        last.then_inc(v_ready, 1)

            def transpose_w(n):
                for c in range(NC):
                    for o in range(NC):
                        last = nc.tensor.transpose(psum[:, W_BANK[n], c * D + o * P:c * D + (o + 1) * P],
                                                   raw[n][:, o, c * P:(c + 1) * P], ident[:, :])
                last.then_inc(w_ready, 1)

            pe.wait_ge(zeroed, 1)
            for _ in range(WARM_UP):
                nc.tensor.matmul(psum[:, 7, 0:2 * P], probs[:, 0:P], probs[:, 0:2 * P], start=True, stop=True)
            pe.wait_ge(consts_ready, 4)
            pe.wait_ge(w_loaded["kf"], 16)
            transpose_w("kf")
            pe.wait_ge(w_shifted["q"], 2)
            pe.wait_ge(w_shifted["k"], 2)
            for c in range(NC):
                for o in range(NC):
                    last = nc.tensor.matmul(psum[:, W_BANK["m"], c * D:(c + 1) * D], raw["k"][:, o, c * P:(c + 1) * P],
                                            raw["q"][:, o, :], start=(o == 0), stop=(o == NC - 1))
            last.then_inc(w_ready, 1)
            transpose_x(0, first=True)
            pe.wait_ge(w_shifted["v"], 2)
            transpose_w("v")
            for n in ("r", "vf"):
                pe.wait_ge(w_loaded[n], 16)
                transpose_w(n)
            pe.wait_ge(w_lo_ready, ATTN_W_AT["m"])
            project_t(0, first=True)
            pe.wait_ge(w_lo_ready, ATTN_W_AT["v"])
            project_v(0, first=True)

            def turn(b, following, first=False):
                pe.wait_ge(t_lo_ready, 2 * b + 2)
                for i in SCORE_ORDER:
                    if first and i > 0:
                        pe.wait_ge(w_whole_ready, 4 - i)
                    if i == 1:
                        pe.wait_ge(tanh_ready, 2 * b)
                    if i > 0:
                        last = three_passes(score_tile(i, (i + 1) * P), [
                            (halves(x_hi, x_lo, c, slice(i * P, (i + 1) * P)), halves(t_hi, t_lo, c, slice(0, (i + 1) * P)))
                            for c in range(NC)])
                    else:
                        for c in range(NC):
                            last = nc.tensor.matmul(score_tile(0, P), x_first[:, c, :], t_first[:, c, :],
                                                    start=(c == 0), stop=(c == NC - 1))
                    if i != 1:
                        last.then_inc(scores_ready, 1)
                if following:
                    transpose_x(b + 1)
                if first:
                    pe.wait_ge(mix_w_lo_ready, MIX_W_AT["kf"])
                pe.wait_ge(mixk_lo_ready, b + 1)
                pe.wait_ge(v_lo_ready, 2 * b + 1)
                for o in range(NC):
                    three_passes(psum[:, KEY_BANK[o], :], [
                        (halves(w_hi["kf"], w_lo["kf"], c, slice(o * P, (o + 1) * P)), halves(mixk_hi, mixk_lo, c, slice(0, S)))
                        for c in range(NC)]).then_inc(key_ready, 1)
                pe.wait_ge(v_lo_ready, 2 * b + 2)
                for g, tiles in enumerate(PROB_TILES):
                    if g == 0:
                        pe.wait_ge(exp_ready, 4 * b + 1)
                    if g == 1:
                        pe.wait_ge(exp_ready, 4 * b + 4)
                    for i in tiles:
                        for j in range(i + 1):
                            at = PROB_AT[i] + j * P
                            last = nc.tensor.transpose(psum[:, PROB_BANK[g], at % 512:at % 512 + P],
                                                       probs[:, at:at + P], ident[:, :])
                    last.then_inc(pT_ready, 1)
                if first:
                    pe.wait_ge(mix_w_lo_ready, MIX_W_AT["r"])
                pe.wait_ge(mixr_lo_ready, b + 1)
                for i in range(NT):
                    if following and i == 2:
                        pe.wait_ge(x_hi_ready, 2 * b + 3)
                    last = three_passes(tile_of(GATE_BANK, i), [
                        (halves(mixr_hi, mixr_lo, c, slice(i * P, (i + 1) * P)), halves(w_hi["r"], w_lo["r"], c, slice(0, D)))
                        for c in range(NC)])
                    if i % 2 == 1:
                        last.then_inc(gate_ready, 1)
                if following:
                    pe.wait_ge(x_hi_ready, 2 * b + 4)
                pe.wait_ge(relu_ready, 2 * b + 2)
                for n, i in enumerate((3, 2, 0, 1)):
                    if i > 0:
                        pe.wait_ge(pT_lo_ready, 3 * b + (3, 2, 1)[i - 1])
                    last = three_passes(tile_of(ATTN_BANK, i), [
                        ((pT_hi[:, PROB_AT[i] + j * P:PROB_AT[i] + (j + 1) * P], pT_lo[:, PROB_AT[i] + j * P:PROB_AT[i] + (j + 1) * P]),
                         (v_hi[:, j, :], v_lo[:, j, :])) for j in range(i + 1)])
                    if n % 2 == 1:
                        last.then_inc(attn_ready, 1)
                if first:
                    pe.wait_ge(mix_w_lo_ready, MIX_W_AT["vf"])
                pe.wait_ge(act_lo_ready, 2 * b + 2)
                for i in range(NT):
                    last = three_passes(tile_of(FFN_BANK, i) if following else psum[:, LAST_FFN_BANK[i], 0:D], [
                        (halves(act_hi, act_lo, c, slice(i * P, (i + 1) * P)), halves(w_hi["vf"], w_lo["vf"], c, slice(0, D)))
                        for c in range(NC)])
                    if i % 2 == 1 or not following:
                        last.then_inc(ffn_ready, 1)
                if following:
                    project_t(b + 1)
                    project_v(b + 1)

            turn(0, True, first=True)
            with pe.Fori(*LOOP) as b:
                turn(b, True)
            turn(B - 2, True)
            turn(B - 1, False)

        @block.scalar
        def _(sc):
            for n, w_in in (("q", Wq), ("k", Wk)):
                sc.dma_start(raw[n][:, :, :], w_in.rearrange("(o p) c -> p o c", p=P)).then_inc(w_loaded[n], 16)
            sc.preload_act_table(ACT.Exp)
            for n in ("q", "k", "v"):
                sc.wait_ge(w_loaded[n], 16)
                for o in range(NC):
                    nc.scalar.activation(scratch[n][:, o, :], raw[n][:, o, :], ACT.Copy,
                                         accum_out=row_total[:, QKV[n], o:o + 1]).then_inc(total_ready, 1)

            def whole_x(c):
                nc.scalar.activation(x_first[:, c, :], psum[:, XT_BANK[c], 0:P], ACT.Copy, bias=UNIT)
                nc.scalar.activation(xT[:, c, 1:S + 1], psum[:, XT_BANK[c], :], ACT.Copy).then_inc(xT_copied, 1)

            def upper_x(c):
                nc.scalar.activation(x_hi[:, c, :], psum[:, XT_BANK[c], :], ACT.Copy, bias=UNIT).then_inc(x_hi_ready, 1)

            def copy_x(b):
                sc.wait_ge(mixr_ready, b)
                for c in range(NC):
                    sc.wait_ge(xT_ready, 2 * b + c + 1)
                    whole_x(c)
                    upper_x(c)

            def upper_mix(b, src, dst, src_ready, dst_ready, read):
                sc.wait_ge(src_ready, b + 1)
                sc.wait_ge(read, 2 * b)
                nc.scalar.activation(dst[:, :, :], src[:, :, :], ACT.Copy).then_inc(dst_ready, 1)

            def upper_t(b):
                for d in range(NC):
                    sc.wait_ge(t_ready, 2 * b + d + 1)
                    nc.scalar.activation(t_first[:, d, :], psum[:, T_BANK[d], 0:P], ACT.Copy)
                    nc.scalar.activation(t_hi[:, d, :], psum[:, T_BANK[d], :], ACT.Copy).then_inc(t_hi_ready, 1)

            def upper_v(b):
                for h in range(2):
                    sc.wait_ge(v_ready, 2 * b + h + 1)
                    nc.scalar.activation(v_hi[:, 2 * h:2 * h + 2, :], psum[:, V_BANK[h], :].rearrange("p (t d) -> p t d", d=D),
                                         ACT.Copy).then_inc(v_hi_ready, 1)

            def upper_w(n):
                sc.wait_ge(w_ready, W_AT[n])
                nc.scalar.activation(w_hi[n][:, :, :], by_chunk(n), ACT.Copy, scale=W_SCALE[n]).then_inc(w_hi_ready, 1)

            def whole_w(n):
                nc.scalar.activation(raw[n][:, :, :], by_chunk(n), ACT.Copy, scale=W_SCALE[n]).then_inc(w_whole_ready, 1)

            upper_w("kf")
            whole_w("kf")
            upper_w("m")
            for c in range(NC):
                sc.wait_ge(xT_ready, c + 1)
                upper_x(c)
            for c in range(NC):
                sc.wait_ge(x_lo_ready, c + 1)
                whole_x(c)
            upper_w("v")
            upper_t(0)
            upper_w("r")
            whole_w("r")
            upper_w("vf")
            whole_w("vf")
            upper_v(0)
            upper_mix(0, mixk, mixk_hi, mixk_ready, mixk_hi_ready, key_ready)
            upper_mix(0, mixr, mixr_hi, mixr_ready, mixr_hi_ready, gate_ready)

            def turn(b, following):
                for n, i in enumerate(SCORE_ORDER):
                    sc.wait_ge(max_ready, 3 * b + min(n, 2) + 1)
                    nc.scalar.activation(probs[:, PROB_AT[i]:PROB_AT[i] + (i + 1) * P], score_tile(i, (i + 1) * P), ACT.Exp,
                                         bias=neg_max[:, i:i + 1], accum_out=row_sum[:, i:i + 1]).then_inc(exp_ready, 1)
                if following:
                    copy_x(b + 1)
                sc.wait_ge(act_ready, 2 * b)
                for o in range(NC):
                    sc.wait_ge(key_ready, 2 * b + o + 1)
                    nc.scalar.activation(relu[:, o, :], psum[:, KEY_BANK[o], :], ACT.Relu).then_inc(relu_ready, 1)
                for g, (lo, hi) in enumerate(PROB_GROUPS):
                    sc.wait_ge(pT_ready, 3 * b + g + 1)
                    nc.scalar.activation(pT_hi[:, lo:hi], psum[:, PROB_BANK[g], 0:hi - lo], ACT.Copy).then_inc(pT_hi_ready, 1)
                for o in range(NC):
                    sc.wait_ge(act_ready, 2 * b + o + 1)
                    nc.scalar.activation(act_hi[:, o, :], act[:, o, :], ACT.Copy).then_inc(act_hi_ready, 1)
                sc.wait_ge(ffn_gated, 2 * b)
                for h in range(2):
                    sc.wait_ge(gate_ready, 2 * b + h + 1)
                    nc.scalar.activation(gate[:, 2 * h:2 * h + 2, :], psum[:, GATE_BANK[h], :].rearrange("p (t d) -> p t d", d=D),
                                         ACT.Tanh, scale=0.5).then_inc(tanh_ready, 1)
                if following:
                    upper_mix(b + 1, mixk, mixk_hi, mixk_ready, mixk_hi_ready, key_ready)
                    upper_mix(b + 1, mixr, mixr_hi, mixr_ready, mixr_hi_ready, gate_ready)
                    upper_t(b + 1)
                    upper_v(b + 1)

            turn(0, True)
            with sc.Fori(*LOOP) as b:
                turn(b, True)
            turn(B - 2, True)
            turn(B - 1, False)

        @block.vector
        def _(dv):
            def statistics(b, loaded):
                for t in range(NT):
                    loaded(t)
                    nc.vector.bn_stats(stats[:, t, :], x_all[:, b, t, :]).then_inc(stats_ready, 1)

            def aggregate(b):
                for t in range(NT):
                    nc.vector.bn_aggr(mv[:, t, :], stats[:, t, :]).then_inc(mv_ready, 1)
                dv.wait_ge(mv_ready, 4 * b + 4)
                nc.vector.tensor_scalar(var_eps[:, :], mv[:, :, 1], EPS, None, ALU.add).then_inc(var_ready, 1)

            def normalise(b, tiles=range(NT)):
                if 0 in tiles:
                    dv.wait_ge(rstd_ready, b + 1)
                    dv.wait_ge(xT_ready, 2 * b)
                for t in tiles:
                    nc.vector.tensor_scalar(xn[:, t, :], x_all[:, b, t, :], mv[:, t, 0:1], rstd[:, t:t + 1],
                                            ALU.subtract, ALU.mult).then_inc(xn_ready, 1)

            def difference(b):
                dv.wait_ge(xT_copied, 2 * b + 2)
                nc.vector.tensor_tensor(diff[:, :, :], xT[:, :, 1:S + 1], xT[:, :, 0:S], ALU.subtract).then_inc(diff_ready, 1)

            def lower_x(b, whole):
                for c in range(NC):
                    dv.wait_ge(x_hi_ready, 2 * b + c + 1)
                    nc.vector.scalar_tensor_tensor(out=x_lo[:, c, :], in0=whole(c), scalar=UNIT, in1=f32(x_hi[:, c, :]),
                                                   op0=ALU.add, op1=ALU.subtract).then_inc(x_lo_ready, 1)

            def mix(b, m, dst, ready, lo_ready):
                dv.wait_ge(diff_ready, b + 1)
                dv.wait_ge(lo_ready, b)
                for c in range(NC):
                    last = nc.vector.scalar_tensor_tensor(out=dst[:, c, :], in0=diff[:, c, :], scalar=mu[m][:, c:c + 1],
                                                          in1=xT[:, c, 0:S], op0=ALU.mult, op1=ALU.add)
                last.then_inc(ready, 1)

            def lower_t(b, chunks=range(NC)):
                for d in chunks:
                    dv.wait_ge(t_hi_ready, 2 * b + d + 1)
                    nc.vector.tensor_tensor(t_lo[:, d, :], psum[:, T_BANK[d], :], f32(t_hi[:, d, :]),
                                            ALU.subtract).then_inc(t_lo_ready, 1)

            def lower_v(b):
                for h in range(2):
                    dv.wait_ge(v_hi_ready, 2 * b + h + 1)
                    nc.vector.tensor_tensor(v_lo[:, 2 * h:2 * h + 2, :], psum[:, V_BANK[h], :].rearrange("p (t d) -> p t d", d=D),
                                            f32(v_hi[:, 2 * h:2 * h + 2, :]), ALU.subtract).then_inc(v_lo_ready, 1)

            def lower_w(n):
                dv.wait_ge(w_hi_ready, W_AT[n])
                nc.vector.tensor_tensor(w_lo[n][:, :, :], by_chunk(n), f32(w_hi[n][:, :, :]),
                                        ALU.subtract).then_inc(w_lo_ready, 1)

            def prepare(names, at):
                these = slice(QKV[names[0]], QKV[names[-1]] + 1)
                dv.wait_ge(total_ready, NC * (QKV[names[-1]] + 1))
                nc.vector.tensor_scalar(neg_mean_w[:, these, :], row_total[:, these, :], -1.0 / D, None, ALU.mult).then_inc(mean_ready, 1)
                for n in names:
                    dv.wait_ge(b_loaded[n], 16)
                dv.wait_ge(mean_ready, at)
                nc.vector.scalar_tensor_tensor(out=shift[:, these, :], in0=bias[:, these, :], scalar=UNIT,
                                               in1=neg_mean_w[:, these, :], op0=ALU.mult, op1=ALU.add).then_inc(shift_ready, 1)
                dv.wait_ge(shift_ready, at)
                for n in names:
                    for o in range(NC):
                        nc.vector.tensor_scalar(raw[n][:, o, :], raw[n][:, o, :], shift[:, QKV[n], o:o + 1],
                                                UNIT if n == "q" else 1.0, ALU.add, ALU.mult).then_inc(w_shifted[n], 1)

            statistics(0, lambda t: dv.wait_ge(x0_loaded[t // 2], 16))
            dv.wait_ge(stats_ready, 4)
            aggregate(0)
            prepare(("q", "k"), 1)
            normalise(0)
            dv.wait_ge(consts_ready, 4)
            prepare(("v",), 2)
            lower_w("m")
            lower_x(0, lambda c: psum[:, XT_BANK[c], :])
            statistics(1, lambda t: dv.wait_ge(x_loaded, 16))
            lower_w("v")
            dv.wait_ge(stats_ready, 8)
            aggregate(1)
            lower_t(0, (0,))
            dv.wait_ge(mu_loaded, 32)
            mix(0, "k", mixk, mixk_ready, mixk_lo_ready)
            lower_t(0, (1,))
            mix(0, "r", mixr, mixr_ready, mixr_lo_ready)
            normalise(1)
            lower_v(0)

            def turn(b, following, after_next):
                for n, i in enumerate(SCORE_ORDER):
                    if i > 0:
                        dv.wait_ge(scores_ready, 3 * b + n + 1)
                        bank, at = SCORES[i]
                        diagonal = psum[:, bank, at + i * P:at + (i + (1 if i > 1 else 2)) * P]
                        nc.vector.tensor_tensor(diagonal, diagonal, mask[:, 0:P if i > 1 else 2 * P], ALU.add).then_inc(masked, 1)
                        dv.wait_ge(masked, 3 * b + n + 1)
                    last = nc.vector.tensor_reduce(neg_max[:, i:i + 1], score_tile(i, (i + 1) * P), AX.X, ALU.max,
                                                   negate=True)
                    if i != 1:
                        last.then_inc(max_ready, 1)
                if after_next:
                    statistics(b + 2, lambda t: dv.wait_ge(x_loaded, 16 * b + 32) if t == 0 else None)
                    dv.wait_ge(stats_ready, 4 * b + 12)
                dv.wait_ge(exp_ready, 4 * b + 4)
                nc.vector.reciprocal(inv_sum[:, :], row_sum[:, :]).then_inc(inv_ready, 1)
                if after_next:
                    aggregate(b + 2)
                if following:
                    difference(b + 1)
                if after_next:
                    normalise(b + 2, (0, 1))
                for g, (lo, hi) in enumerate(PROB_GROUPS):
                    dv.wait_ge(pT_hi_ready, 3 * b + g + 1)
                    nc.vector.tensor_tensor(pT_lo[:, lo:hi], psum[:, PROB_BANK[g], 0:hi - lo], f32(pT_hi[:, lo:hi]),
                                            ALU.subtract).then_inc(pT_lo_ready, 1)
                if after_next:
                    normalise(b + 2, (2, 3))
                if following:
                    lower_x(b + 1, lambda c: xT[:, c, 1:S + 1])
                    mix(b + 1, "k", mixk, mixk_ready, mixk_lo_ready)
                    mix(b + 1, "r", mixr, mixr_ready, mixr_lo_ready)
                dv.wait_ge(inv_ready, b + 1)
                dv.wait_ge(y_ready, 2 * b)
                for n, i in enumerate((3, 2, 0, 1)):
                    dv.wait_ge(attn_ready, 2 * b + n // 2 + 1)
                    nc.vector.scalar_tensor_tensor(out=attn[:, i, :], in0=tile_of(ATTN_BANK, i), scalar=inv_sum[:, i:i + 1],
                                                   in1=x_all[:, b, i, :], op0=ALU.mult, op1=ALU.add).then_inc(attn_added, 1)
                dv.wait_ge(tanh_ready, 2 * b + 2)
                if following:
                    for h in range(2):
                        two = slice(2 * h, 2 * h + 2)
                        dv.wait_ge(ffn_ready, 2 * b + h + 1)
                        nc.vector.scalar_tensor_tensor(out=ffn[:, two, :], in0=gate[:, two, :], scalar=1.0,
                                                       in1=psum[:, FFN_BANK[h], :].rearrange("p (t d) -> p t d", d=D),
                                                       op0=ALU.add, op1=ALU.mult).then_inc(ffn_gated, 1)
                else:
                    dv.wait_ge(attn_added, 4 * b + 4)
                    dv.wait_ge(y_stored, 16 * b)
                    for i in range(NT):
                        dv.wait_ge(ffn_ready, 2 * b + i + 1)
                        nc.vector.scalar_tensor_tensor(out=ffn[:, i, :], in0=gate[:, i, :], scalar=1.0,
                                                       in1=psum[:, LAST_FFN_BANK[i], 0:D],
                                                       op0=ALU.add, op1=ALU.mult).then_inc(ffn_gated, 1)
                        dv.wait_ge(ffn_gated, 2 * b + i + 1)
                        nc.vector.tensor_tensor(y[:, i, :], attn[:, i, :], ffn[:, i, :], ALU.add).then_inc(y_ready, 1)
                if following:
                    lower_t(b + 1)
                    lower_v(b + 1)

            turn(0, True, True)
            with dv.Fori(*LOOP) as b:
                turn(b, True, True)
            turn(B - 2, True, False)
            turn(B - 1, False, False)

        @block.gpsimd
        def _(gp):
            def load_bias(n, b_in):
                gp.dma_start(bias[:, QKV[n], :], b_in.rearrange("(o p) -> p o", p=P),
                             allow_slow_non_contiguous=True).then_inc(b_loaded[n], 16)

            gp.memset(probs[:, 0:2 * P], 0.0).then_inc(zeroed, 1)
            gp.memset(neg_half[:, :], -0.5).then_inc(consts_ready, 1)
            gp.memset(xT[:, :, 0:1], 0.0).then_inc(consts_ready, 1)
            load_bias("q", bq)
            load_bias("k", bk)
            load_bias("v", bv)
            for tile in (ident, mask):
                gp.memset(tile[:, :], 0.0).then_inc(zeroed, 1)
            gp.wait_ge(zeroed, 3)
            gp.affine_select(out=ident[:, :], in_=ident[:, :], compare_op=ALU.not_equal, fill=1.0, base=0,
                             pattern=[[-1, P]], channel_multiplier=1).then_inc(consts_ready, 1)
            causal = mask[:, :].rearrange("p (a k) -> p a k", k=P)
            gp.affine_select(out=causal, in_=causal, compare_op=ALU.is_ge, fill=MASKED, base=0,
                             pattern=[[0, 2], [-1, P]], channel_multiplier=1).then_inc(consts_ready, 1)

            def inverse_deviation(b):
                gp.wait_ge(var_ready, b + 1)
                nc.gpsimd.tensor_tensor(rstd[:, :], var_eps[:, :], neg_half[:, :], ALU.pow).then_inc(rstd_ready, 1)

            def lower(b, whole, hi, lo, hi_ready, lo_ready):
                gp.wait_ge(hi_ready, b + 1)
                nc.gpsimd.tensor_tensor(lo[:, :, :], whole[:, :, :], f32(hi[:, :, :]), ALU.subtract).then_inc(lo_ready, 1)

            inverse_deviation(0)
            for n, m_in in (("k", mu_k), ("r", mu_r)):
                gp.dma_start(mu[n][:, :], m_in.rearrange("(c p) -> p c", p=P), allow_slow_non_contiguous=True).then_inc(mu_loaded, 16)

            def lower_w(n):
                gp.wait_ge(w_whole_ready, MIX_W_AT[n])
                nc.gpsimd.tensor_tensor(w_lo[n][:, :, :], raw[n][:, :, :], f32(w_hi[n][:, :, :]),
                                        ALU.subtract).then_inc(mix_w_lo_ready, 1)

            lower_w("kf")
            for c in range(NC):
                gp.wait_ge(xT_copied, c + 1)
                last = nc.gpsimd.tensor_tensor(diff[:, c, :], xT[:, c, 1:S + 1], xT[:, c, 0:S], ALU.subtract)
            last.then_inc(diff_ready, 1)
            inverse_deviation(1)
            lower_w("r")
            lower(0, mixk, mixk_hi, mixk_lo, mixk_hi_ready, mixk_lo_ready)
            lower_w("vf")
            lower(0, mixr, mixr_hi, mixr_lo, mixr_hi_ready, mixr_lo_ready)

            def turn(b, following, after_next):
                if after_next:
                    inverse_deviation(b + 2)
                for o in range(NC):
                    gp.wait_ge(relu_ready, 2 * b + o + 1)
                    if o == 0:
                        gp.wait_ge(act_hi_ready, 2 * b)
                        gp.wait_ge(act_lo_ready, 2 * b)
                    nc.gpsimd.tensor_tensor(act[:, o, :], relu[:, o, :], relu[:, o, :], ALU.mult).then_inc(act_ready, 1)
                for o in range(NC):
                    gp.wait_ge(act_hi_ready, 2 * b + o + 1)
                    nc.gpsimd.tensor_tensor(act_lo[:, o, :], act[:, o, :], f32(act_hi[:, o, :]),
                                            ALU.subtract).then_inc(act_lo_ready, 1)
                if following:
                    lower(b + 1, mixk, mixk_hi, mixk_lo, mixk_hi_ready, mixk_lo_ready)
                    lower(b + 1, mixr, mixr_hi, mixr_lo, mixr_hi_ready, mixr_lo_ready)
                    gp.wait_ge(attn_added, 4 * b + 4)
                    gp.wait_ge(y_stored, 16 * b)
                    for h in range(2):
                        two = slice(2 * h, 2 * h + 2)
                        gp.wait_ge(ffn_gated, 2 * b + h + 1)
                        nc.gpsimd.tensor_tensor(y[:, two, :], attn[:, two, :], ffn[:, two, :], ALU.add).then_inc(y_ready, 1)

            turn(0, True, True)
            with gp.Fori(*LOOP) as b:
                turn(b, True, True)
            turn(B - 2, True, False)
            turn(B - 1, False, False)


_INS = ["L0_attn_x", "L0_attn_Wk", "L0_attn_bk", "L0_attn_Wq", "L0_attn_bq", "L0_attn_Wv", "L0_attn_bv",
        "L0_ffn_W_r", "L0_ffn_W_k", "L0_ffn_W_v", "L0_ffn_mu_r", "L0_ffn_mu_k"]


def kernel(**inputs):
    import numpy as _np
    import concourse.bacc as _bacc
    from concourse import mybir as _mybir
    from concourse.bass_utils import run_bass_kernel_spmd as _run

    nc = _bacc.Bacc("TRN2", target_bir_lowering=False, num_devices=1)
    arrays, args = {}, []
    for name in _INS:
        a = _np.ascontiguousarray(inputs[name])
        arrays[f"in_{name}"] = a
        args.append(nc.dram_tensor(f"in_{name}", a.shape, _mybir.dt.from_np(a.dtype), kind="ExternalInput").ap())
    out = nc.dram_tensor("out_0", inputs["L0_attn_x"].shape, _mybir.dt.float32, kind="ExternalOutput").ap()
    attention_and_channel_mix_kernel(nc, *args, out)
    r = _run(nc, [arrays], core_ids=[0])
    return r.results[0]["out_0"]
```
